# Optimizing a Trainium2 kernel written in Bass

```python
import numpy as np
import jax
import jax.numpy as jnp

def _softmax(x, axis=-1):
    return jax.nn.softmax(x, axis=axis)

def _gelu(x):
    return jax.nn.gelu(x, approximate=True)

def _silu(x):
    return jax.nn.silu(x)

def _sigmoid(x):
    return jax.nn.sigmoid(x)

def _layernorm(x, axis=-1, eps=1e-05):
    m = jnp.mean(x, axis=axis, keepdims=True)
    v = jnp.var(x, axis=axis, keepdims=True)
    return (x - m) / jnp.sqrt(v + eps)

def _scatter_add(tgt, idx, src, axis=0):
    return tgt.at[idx].add(src)

def _segment_sum(src, seg, n):
    return jax.ops.segment_sum(src, seg, n)
kernel_name = 'mk_gnn_resnorm_d2_gnn_r16_177302'

def setup_inputs(seed: int=0):
    np.random.seed(seed)
    _w = jnp.asarray

    def _rec_inputs():
        import jax
        import jax.numpy as jnp
        _gk = jax.random.key(seed)
        x = -0.0001126 + 1 * jax.random.normal(jax.random.fold_in(_gk, 1), (6250, 256), jnp.float32)
        src = jax.random.randint(jax.random.fold_in(_gk, 2), (100000,), 0, 6250, jnp.int32)
        dst = jax.random.randint(jax.random.fold_in(_gk, 3), (100000,), 0, 6250, jnp.int32)
        _o = jnp.argsort(dst, stable=True)
        src = src[_o]
        dst = dst[_o]
        return (x, src, dst)
    x, src, dst = _rec_inputs()

    def _L0_gnn_setup():
        import jax, jax.numpy as jnp
        import numpy as np
        H, C = (4, 64)
        NEG_SLOPE = 0.2

        def _gatv2_layer(x, src, dst, n, Wl, Wr, att, b):
            xl = (x @ Wl).reshape(n, H, C)
            xr = (x @ Wr).reshape(n, H, C)
            e = jax.nn.leaky_relu(xl[src] + xr[dst], NEG_SLOPE)
            logits = jnp.einsum('ehc,hc->eh', e, att)
            m = jax.ops.segment_max(logits, dst, num_segments=n)
            ex = jnp.exp(logits - m[dst])
            denom = jax.ops.segment_sum(ex, dst, num_segments=n)
            alpha = ex / (denom[dst] + 1e-16)
            msg = xl[src] * alpha[:, :, None]
            out = jax.ops.segment_sum(msg, dst, num_segments=n)
            return out.reshape(n, H * C) + b
        key = jax.random.key(seed)
        ks = jax.random.split(key, 10)
        N, E, F = (1875, 30000, 256)
        x = jax.random.normal(ks[0], (N, F), dtype=jnp.float32)
        edge_index = jax.random.randint(ks[1], (2, E), 0, N, dtype=jnp.int64)
        s = 1.0 / np.sqrt(F)

        def w(k, shape):
            return jax.random.uniform(k, shape, jnp.float32, -s, s)
        return {'x': x, 'edge_index': edge_index, 'Wl1': w(ks[2], (F, H * C)), 'Wr1': w(ks[3], (F, H * C)), 'att1': w(ks[4], (H, C)), 'b1': jnp.zeros((H * C,), jnp.float32), 'Wl2': w(ks[5], (F, H * C)), 'Wr2': w(ks[6], (F, H * C)), 'att2': w(ks[7], (H, C)), 'b2': jnp.zeros((H * C,), jnp.float32)}
    _L0_gnn_all = _L0_gnn_setup()
    _L0_gnn_in = {k: v for k, v in _L0_gnn_all.items() if k in ('Wl1', 'Wr1', 'att1', 'b1', 'Wl2', 'Wr2', 'att2', 'b2')}
    del _L0_gnn_all

    def _L1_gnn_setup():
        import jax, jax.numpy as jnp
        import numpy as np
        ALPHA = 0.2
        N_NODES, N_EDGES, N_FEAT, N_HID, N_HEADS = (3125, 50000, 256, 32, 8)
        key = jax.random.key(seed)
        k_h, k_w, k_a, k_s, k_d = jax.random.split(key, 5)
        h = jax.random.normal(k_h, (N_NODES, N_FEAT), dtype=jnp.float32)
        W = jax.random.normal(k_w, (N_HEADS, N_FEAT, N_HID), dtype=jnp.float32) * 0.05
        a = jax.random.normal(k_a, (N_HEADS, 2 * N_HID), dtype=jnp.float32) * 0.05
        src = jax.random.randint(k_s, (N_EDGES,), 0, N_NODES, dtype=jnp.int32)
        dst = jax.random.randint(k_d, (N_EDGES,), 0, N_NODES, dtype=jnp.int32)
        return {'h': h, 'W': W, 'a': a, 'src': src, 'dst': dst}
    _L1_gnn_all = _L1_gnn_setup()
    _L1_gnn_in = {k: v for k, v in _L1_gnn_all.items() if k in ('W', 'a')}
    del _L1_gnn_all
    return {'x': x, 'src': src, 'dst': dst, 'L0_gnn_Wl1': _L0_gnn_in['Wl1'], 'L0_gnn_Wr1': _L0_gnn_in['Wr1'], 'L0_gnn_att1': _L0_gnn_in['att1'], 'L0_gnn_b1': _L0_gnn_in['b1'], 'L0_gnn_Wl2': _L0_gnn_in['Wl2'], 'L0_gnn_Wr2': _L0_gnn_in['Wr2'], 'L0_gnn_att2': _L0_gnn_in['att2'], 'L0_gnn_b2': _L0_gnn_in['b2'], 'L1_gnn_W': _L1_gnn_in['W'], 'L1_gnn_a': _L1_gnn_in['a']}

def reference(x, src, dst, L0_gnn_Wl1, L0_gnn_Wr1, L0_gnn_att1, L0_gnn_b1, L0_gnn_Wl2, L0_gnn_Wr2, L0_gnn_att2, L0_gnn_b2, L1_gnn_W, L1_gnn_a):
    import jax
    import jax.numpy as jnp

    def _L0_gnn_ref(x, edge_index, Wl1, Wr1, att1, b1, Wl2, Wr2, att2, b2):
        import jax, jax.numpy as jnp
        import numpy as np
        H, C = (4, 64)
        NEG_SLOPE = 0.2

        def _gatv2_layer(x, src, dst, n, Wl, Wr, att, b):
            xl = (x @ Wl).reshape(n, H, C)
            xr = (x @ Wr).reshape(n, H, C)
            e = jax.nn.leaky_relu(xl[src] + xr[dst], NEG_SLOPE)
            logits = jnp.einsum('ehc,hc->eh', e, att)
            m = jax.ops.segment_max(logits, dst, num_segments=n)
            ex = jnp.exp(logits - m[dst])
            denom = jax.ops.segment_sum(ex, dst, num_segments=n)
            alpha = ex / (denom[dst] + 1e-16)
            msg = xl[src] * alpha[:, :, None]
            out = jax.ops.segment_sum(msg, dst, num_segments=n)
            return out.reshape(n, H * C) + b
        n = x.shape[0]
        loops = jnp.arange(n, dtype=edge_index.dtype)
        src = jnp.concatenate([edge_index[0], loops])
        dst = jnp.concatenate([edge_index[1], loops])
        h = _gatv2_layer(x, src, dst, n, Wl1, Wr1, att1, b1)
        h = jax.nn.elu(h)
        h = _gatv2_layer(h, src, dst, n, Wl2, Wr2, att2, b2)
        return h

    def _L1_gnn_ref(h, W, a, src, dst):
        import jax, jax.numpy as jnp
        import numpy as np
        ALPHA = 0.2
        N_NODES, N_EDGES, N_FEAT, N_HID, N_HEADS = (3125, 50000, 256, 32, 8)
        N = h.shape[0]
        H, _, D = W.shape
        Wh = jnp.einsum('nf,hfd->hnd', h, W)
        a1, a2 = (a[:, :D], a[:, D:])
        s1 = jnp.einsum('hnd,hd->hn', Wh, a1)
        s2 = jnp.einsum('hnd,hd->hn', Wh, a2)
        e = jax.nn.leaky_relu(s1[:, src] + s2[:, dst], ALPHA)
        seg_max = jax.vmap(lambda x: jax.ops.segment_max(x, dst, num_segments=N))(e)
        ex = jnp.exp(e - seg_max[:, dst])
        denom = jax.vmap(lambda x: jax.ops.segment_sum(x, dst, num_segments=N))(ex)
        attn = ex / denom[:, dst]
        msg = attn[:, :, None] * Wh[:, src]
        out = jax.vmap(lambda m: jax.ops.segment_sum(m, dst, num_segments=N))(msg)
        return jnp.transpose(out, (1, 0, 2)).reshape(N, H * D)
    edge_index = jnp.stack([src, dst])
    x = _layernorm(x + _L0_gnn_ref(x, edge_index, L0_gnn_Wl1, L0_gnn_Wr1, L0_gnn_att1, L0_gnn_b1, L0_gnn_Wl2, L0_gnn_Wr2, L0_gnn_att2, L0_gnn_b2), axis=-1)
    x = _layernorm(x + _L1_gnn_ref(x, L1_gnn_W, L1_gnn_a, src, dst), axis=-1)
    return x

_drawn_inputs = setup_inputs


def setup_inputs(seed=0):
    import zlib

    import numpy as np

    out = dict(_drawn_inputs(seed))
    spreads = {'L0_gnn_b1': (0.0, 0.1), 'L0_gnn_b2': (0.0, 0.1)}
    factors = {'L0_gnn_Wr1': 36.158, 'L0_gnn_att1': 8.0, 'L0_gnn_Wr2': 64.0, 'L0_gnn_att2': 64.0}
    for name, (base, spread) in spreads.items():
        noise = np.random.default_rng([zlib.crc32(name.encode()), seed]).standard_normal(out[name].shape)
        drawn = base * np.exp(spread * noise) if base else spread * noise
        out[name] = jnp.asarray(drawn.astype(out[name].dtype))
    for name, factor in factors.items():
        out[name] = (out[name] * factor).astype(out[name].dtype)
    return out
```

```python
from contextlib import ExitStack

import concourse.bass as bass
from concourse import mybir

P = 128
GI = 16
D = 256
ROW = D + 8
BIG = 1e30
SLOPE = 0.2
EPS = 1e-5

ALU = mybir.AluOpType
ACT = mybir.ActivationFunctionType
AX = mybir.AxisListType
F32 = mybir.dt.float32
BF16 = mybir.dt.bfloat16
I32 = mybir.dt.int32
DVE = mybir.EngineType.DVE
PE = mybir.EngineType.PE


def sizes(n_nodes, n_edges):
    tiles = -(-n_nodes // P)
    chunks = n_edges // P + 1
    while (chunks + tiles - 1) % (2 * GI):
        chunks += 1
    return tiles, chunks, chunks + tiles - 1


def cut(n):
    blocks = next(b for b in range(1, n + 1) if n % b == 0 and n // b <= P)
    return blocks, n // blocks


def gnn_program(nc, x, src, dst, wl1, wr1, att1, b1, wl2, wr2, att2, b2, w_gat, a_gat, out):
    N = out.shape[0]
    CHUNKS = dst.shape[0]
    TILES = x.shape[0] // P
    ITEMS = CHUNKS + TILES - 1
    NG = ITEMS // GI
    NB, BS = cut(ITEMS)
    CB, CS = cut(CHUNKS)
    assert NG % 2 == 0 and NG >= 4 and N % P and TILES >= 4
    FB = 4
    LAST = N - (TILES - 1) * P

    tab = [nc.dram_tensor(f"table{l}", (TILES * P, ROW), F32, kind="Internal").ap() for l in range(3)]
    hx_dram = nc.dram_tensor("hx_dram", (TILES * P, D), F32, kind="Internal").ap()
    rel_dram = nc.dram_tensor("rel_dram", (ITEMS, P), BF16, kind="Internal").ap()
    key_dram = nc.dram_tensor("key_dram", (ITEMS * P + 2,), F32, kind="Internal").ap()
    flag_dram = nc.dram_tensor("flag_dram", (ITEMS, 4 * P), F32, kind="Internal").ap()

    with ExitStack() as ctx:
        def sb(name, shape, dt=F32):
            return ctx.enter_context(nc.sbuf_tensor(name, shape, dt))

        def psum(name, shape):
            return ctx.enter_context(nc.psum_tensor(name, shape, F32))

        def sem(name):
            return ctx.enter_context(nc.semaphore(name))

        x3 = sb("x3", [P, TILES, 3, ROW], BF16)
        scratch_words = 13 * 1024 + 2 * P
        acc_mem = sb("acc_mem", [P, max(TILES * ROW, scratch_words)])
        acc = acc_mem[:, 0:TILES * ROW].rearrange("p (t r) -> p t r", r=ROW)
        G = sb("gathered", [P, 2, GI, ROW])
        src_items = sb("src_items", [P, ITEMS], I32)
        rel_items = sb("rel_items", [P, ITEMS])
        last_items = sb("last_items", [P, ITEMS], BF16)
        t_row = sb("t_row", [1, ITEMS], I32)
        ident = sb("ident", [P, P])
        iota_row = sb("iota_row", [P, P])
        iota_part = sb("iota_part", [P, 1])
        ones = sb("ones", [P, P])
        ones_b = sb("ones_b", [P, 1], BF16)
        zeros = sb("zeros", [P, ROW])
        idx = sb("idx", [P, 2, GI], I32)
        DT = sb("DT", [P, 2, GI * P], BF16)
        Dm = sb("Dm", [P, 4, P])
        Z = sb("Z", [P, 2, D])
        reluT = sb("reluT", [P, 2, D])
        exs = sb("exs", [P, 2, GI, 8])
        flags = sb("flags", [P, 2, 4, P])
        F1 = sb("F1", [P, P])
        B1 = sb("B1", [P, P])
        mT = sb("mT", [P, P])
        lr = sb("lr", [P, P])
        cand = sb("cand", [P, P])
        dif = sb("dif", [P, P])
        dself = sb("dself", [P, P])
        arow = sb("arow", [1, 4, 8 * (GI + 1)])
        Fout = sb("Fout", [1, 8 * (GI + 1)])
        Bout = sb("Bout", [1, 8 * (GI + 1)])
        carry_in = sb("carry_in", [1, 2, 8 * GI])
        fr = sb("fr", [1, 3, 8])
        onehot0 = sb("onehot0", [P, 2])
        resc = sb("resc", [P, 8])
        attblk = sb("attblk", [P, 2, 4])
        g_at = [0]

        def in_g(*shape):
            words = 1
            for n in shape:
                words *= n
            a = G[:].rearrange("p b i r -> p (b i r)")[:, g_at[0]:g_at[0] + words]
            g_at[0] += words
            return a if len(shape) == 1 else a.rearrange("p (a c) -> p a c", a=shape[0])

        W = in_g(2, 544)
        attb = in_g(2, D)
        bias = in_g(D)
        wtmp = in_g(D)
        hbuf = in_g(2, D)
        hT = in_g(2, D)
        r1 = in_g(ROW)
        zs = in_g(D)
        own = in_g(2, ROW)
        res = in_g(2, D)
        tmp = in_g(D)
        ex = in_g(D)
        xls = sb("xls", [P, 2, ROW])
        xr = sb("xr", [P, 2, ROW])
        small = sb("small", [P, 8, 8])
        pool_pad = sb("pool_pad", [P, 1])
        pX = psum("pX", [P, 2, 512])
        pZ = psum("pZ", [P, 2, 512])
        pS = psum("pS", [P, 2, 512])
        pL = psum("pL", [P, 512])
        pM = psum("pM", [P, 512])

        at = [0]

        def carve(words):
            a = acc_mem[:, at[0]:at[0] + words]
            at[0] += words
            assert at[0] <= acc_mem.shape[1]
            return a

        g_src = carve(NB * P).bitcast(I32)[0:BS].rearrange("p (b e) -> p b e", b=NB)
        g_dst = carve(NB * P).bitcast(I32)[0:BS].rearrange("p (b e) -> p b e", b=NB)
        dstf = carve(NB * P)[0:BS].rearrange("p (b e) -> p b e", b=NB)
        rel = carve(NB * P)[0:BS].rearrange("p (b e) -> p b e", b=NB)
        key = carve(NB * P)[0:BS].rearrange("p (b e) -> p b e", b=NB)
        prev = carve(NB * P)[0:BS].rearrange("p (b e) -> p b e", b=NB)
        nxt = carve(NB * P)[0:BS].rearrange("p (b e) -> p b e", b=NB)
        flg = carve(NB * 4 * P)[0:BS].rearrange("p (b f e) -> p b f e", b=NB, f=4)
        relbf = carve(NB * P // 2).bitcast(BF16)[0:BS].rearrange("p (b e) -> p b e", b=NB)
        srcf, lastf = prev, dstf
        KI = max(ITEMS, P)
        iota_k_i = carve(KI).bitcast(I32)
        kbig = carve(KI)
        cols = carve(16 * 8)
        cmp = x3[:].rearrange("p t s r -> p (t s r)") if CB * ITEMS <= TILES * 3 * ROW else sb("cmp", [P, CB * ITEMS], BF16)[:]
        cmp = cmp[0:CS, 0:CB * ITEMS].rearrange("p (j k) -> p j k", j=CB)
        kf = sb("kf", [P, 16])
        ki = sb("ki", [P, 3, 16], I32)

        pre_ld = sem("pre_ld")
        pre_iota = sem("pre_iota")
        pre_ones = sem("pre_ones")
        pre_v = sem("pre_v")
        pre_pe = sem("pre_pe")
        pre_act = sem("pre_act")
        pre_gather = sem("pre_gather")
        pre_rel = sem("pre_rel")
        pre_key = sem("pre_key")
        pre_shift = sem("pre_shift")
        pre_flag = sem("pre_flag")
        pre_acc = sem("pre_acc")
        w_in = sem("w_in")
        att_in = sem("att_in")
        w_ready = sem("w_ready")
        wchain = sem("wchain")
        h_in = [sem(f"h_in{b}") for b in range(2)]
        own_in = [sem(f"own_in{b}") for b in range(2)]
        res_in = [sem(f"res_in{b}") for b in range(2)]
        h_ready = sem("h_ready")
        h_turned = sem("h_turned")
        ht_ready = sem("ht_ready")
        mm_done = sem("mm_done")
        xls_ready = sem("xls_ready")
        xr_ready = sem("xr_ready")
        self_ready = sem("self_ready")
        split_done = sem("split_done")
        split_step = sem("split_step")
        node_step = sem("node_step")
        elu_in = sem("elu_in")
        elu_exp = sem("elu_exp")
        var_ready = sem("var_ready")
        std_ready = sem("std_ready")
        acc_read = sem("acc_read")
        stored = [sem(f"stored{b}") for b in range(2)]
        hx_stored = [sem(f"hx_stored{b}") for b in range(2)]
        out_stored = [sem(f"out_stored{b}") for b in range(2)]
        landed = [[sem(f"landed{b}_{i}") for i in range(GI)] for b in range(2)]
        x_done = sem("x_done")
        z_done = sem("z_done")
        exs_done = sem("exs_done")
        zt_done = sem("zt_done")
        relu_done = sem("relu_done")
        log_done = sem("log_done")
        wg_done = sem("wg_done")
        seg_done = sem("seg_done")
        acc_done = sem("acc_done")
        idx_ready = sem("idx_ready")
        relb_in = [sem(f"relb_in{b}") for b in range(2)]
        flags_in = [[sem(f"flags_in{h}_{b}") for b in range(2)] for h in (4, 8)]
        dt_ready = sem("dt_ready")
        s_l1, s_l2, s_cand, s_lt, s_scan, s_ab, s_arow, s_car, s_carc, s_t, s_m, s_me = (
            sem(n) for n in ("s_l1", "s_l2", "s_cand", "s_lt", "s_scan", "s_ab", "s_arow", "s_car",
                             "s_carc", "s_t", "s_m", "s_me"))
        s_fr, s_d, s_fx, s_w, s_ws, s_fb, s_wl, s_oh, s_noh, s_sc, s_resc, s_cp = (
            sem(n) for n in ("s_fr", "s_d", "s_fx", "s_w", "s_ws", "s_fb", "s_wl", "s_oh", "s_noh",
                             "s_sc", "s_resc", "s_cp"))

        s_cin = sem("s_cin")

        block = ctx.enter_context(nc.Block())

        def heads(l):
            return 8 if l == 2 else 4

        def flags_need(l, gh, b):
            H = heads(l)
            n = gh + 1 + (l * (NG // 2) if l < 2 else 0)
            return flags_in[l // 2][b], n * (16 * H)

        def landed_need(l, gh):
            return (gh + (l * (NG // 2) + 1)) * 16

        def groups(eng, l, body):
            body(0, 0, True, False)
            if l == 0:
                body(0, 1, True, True)
                body(1, 0, True, True)
            with eng.Fori(1 if l == 0 else 0, NG // 2 - 1) as j:
                body(j, 1, True, True)
                body(j + 1, 0, True, True)
            body(NG // 2 - 1, 1, True, True)
            body(NG // 2, 0, False, True)

        def tiles(eng, body):
            with eng.Fori(0, TILES // 2) as j:
                body(j * 2, 0)
                body(j * 2 + 1, 1)
            if TILES % 2:
                body(TILES - 1, 0)

        def static(v):
            return isinstance(v, int)

        def per_h(ap, H):
            return ap[:, 0:GI * H].rearrange("p (h i) -> p i h", h=H)

        SECOND = {7: (0, 1), 8: (2, 3), 9: (4, 5), 10: (6, 7), 11: (8, 9), 12: (10, 11), 13: (12, 13), 14: (14,), 15: (15,)}

        @block.sync
        def _(sp):
            with nc.allow_non_contiguous_dma(reason="one column of dst, once"):
                sp.dma_start(ki[0:CS, 0, 0:CB], dst[:, P - 1:P].rearrange("(j p) o -> p (j o)", p=CS)).then_inc(pre_ld, 16)

            def weights(l):
                if l > 0:
                    sp.wait_ge(acc_done, l * NG * GI)
                with nc.allow_non_contiguous_dma(reason="small weights"):
                    if l < 2:
                        wl, wr, att = ((wl1, wr1, att1), (wl2, wr2, att2))[l]
                        sp.dma_start(W[:, :, 0:D], wl.rearrange("(q p) n -> p q n", p=P)).then_inc(w_in, 16)
                        sp.dma_start(W[:, :, D + 4:2 * D + 4], wr.rearrange("(q p) n -> p q n", p=P)).then_inc(w_in, 16)
                        sp.dma_start(attb[:, 0, :], att.rearrange("h c -> (h c)").partition_broadcast(P)).then_inc(w_in, 16)
                    else:
                        for q in range(2):
                            sp.dma_start(W[:, q, 0:D].rearrange("p (h d) -> p h d", h=8),
                                         w_gat[:, q * P:(q + 1) * P, :].rearrange("h p d -> p h d")).then_inc(w_in, 16)
                        for s in range(2):
                            sp.dma_start(attb[:, s, :].rearrange("p (h d) -> p h d", h=8),
                                         a_gat[:, s * 32:(s + 1) * 32].partition_broadcast(P)).then_inc(w_in, 16)
                    if l > 0:
                        sp.dma_start(bias, (b1, b2)[l - 1].partition_broadcast(P)).then_inc(w_in, 16)

            def attention_blocks(l):
                att = (att1, att2)[l]
                with nc.allow_non_contiguous_dma(reason="256 attention weights as columns"):
                    for h in range(4):
                        r, q = h % 2, h // 2
                        sp.dma_start(attblk[r * 64:(r + 1) * 64, q, h:h + 1],
                                     att[h:h + 1, :].rearrange("o c -> c o")).then_inc(att_in, 16)

            def rows(t):
                return bass.ds(t * P, P)

            def node_loads(l):
                def body(t, b):
                    T = t + l * TILES
                    first = l == 0 and static(t) and t < 2
                    if l == 0:
                        sp.wait_ge(h_turned, T + 1)if False else None
                        sp.dma_start(hbuf[:, b, :], x[rows(t), :]).then_inc(h_in[b], 16)
                    if l in (1, 2):
                        sp.dma_start(own[:, b, :], tab[l - 1][rows(t), :]).then_inc(own_in[b], 16)
                    if l in (2, 3):
                        sp.dma_start(res[:, b, :], (x if l == 2 else hx_dram)[rows(t), :]).then_inc(res_in[b], 16)

                def waits(t, b):
                    if l == 0:
                        sp.wait_ge(h_turned, t - 1)
                    else:
                        sp.wait_ge(acc_read, t - 1 + (l - 1) * TILES)

                body(0, 0)
                body(1, 1)
                with sp.Fori(1, TILES // 2) as j:
                    waits(j * 2, 0)
                    body(j * 2, 0)
                    waits(j * 2 + 1, 1)
                    body(j * 2 + 1, 1)
                if TILES % 2:
                    waits(TILES - 1, 0)
                    body(TILES - 1, 0)

            def group_loads(l):
                H = heads(l)

                def body(gh, b):
                    G1 = gh * 2 + (b + l * NG)
                    if not (static(G1) and G1 < 2):
                        sp.wait_ge(s_oh, G1 - 1)
                    k0 = (gh * 2 + b) * GI
                    sp.dma_start(DT[:, b, :], rel_dram[bass.ds(k0, GI), :].rearrange("k e -> (k e)").partition_broadcast(P)).then_inc(relb_in[b], 16)
                    if not (static(G1) and G1 < 2):
                        sp.wait_ge(s_m, G1 - 1)
                    for h in range(H):
                        sp.dma_start(flags[h * GI:(h + 1) * GI, b].rearrange("p f e -> p (f e)"),
                                     flag_dram[bass.ds(k0, GI), :]).then_inc(flags_in[l // 2][b], 16)

                body(0, 0)
                body(0, 1)
                with sp.Fori(1, NG // 2) as j:
                    body(j, 0)
                    body(j, 1)

            weights(0)
            sp.wait_ge(pre_ones, 1)
            attention_blocks(0)
            sp.wait_ge(pre_v, PV_REL)
            sp.dma_start(rel_dram.rearrange("(b p) e -> p b e", p=BS), relbf).then_inc(pre_rel, 16)
            flat = key_dram[1:1 + ITEMS * P].rearrange("(b p e) -> p b e", p=BS, e=P)
            sp.dma_start(flat, key).then_inc(pre_key, 16)
            sp.dma_start(key_dram[0:1], zeros[0:1, 0:1]).then_inc(pre_key, 16)
            sp.dma_start(key_dram[1 + ITEMS * P:2 + ITEMS * P], zeros[0:1, 0:1]).then_inc(pre_key, 16)
            sp.wait_ge(pre_key, 48)
            sp.wait_ge(pre_act, 3)
            sp.dma_start(prev, key_dram[0:ITEMS * P].rearrange("(b p e) -> p b e", p=BS, e=P)).then_inc(pre_shift, 16)
            sp.dma_start(nxt, key_dram[2:2 + ITEMS * P].rearrange("(b p e) -> p b e", p=BS, e=P)).then_inc(pre_shift, 16)
            sp.wait_ge(pre_v, PV_FLAG)
            sp.dma_start(flag_dram.rearrange("(b p) f -> p b f", p=BS), flg.rearrange("p b f e -> p b (f e)")).then_inc(pre_flag, 16)
            node_loads(0)
            sp.wait_ge(pre_rel, 16)
            sp.wait_ge(pre_flag, 16)
            for l in range(3):
                group_loads(l)
                if l < 2:
                    weights(l + 1)
                if l == 0:
                    attention_blocks(1)
                if l == 2:
                    sp.wait_ge(acc_done, 3 * NG * GI)
                    for b in range(2):
                        sp.wait_ge(hx_stored[b], 16 * ((TILES + 1 - b) // 2))
                node_loads(l + 1)

        @block.gpsimd
        def _(pool):
            nc.gpsimd.memset(ones[:], 1.0)
            nc.gpsimd.memset(ones_b[:], 1.0)
            nc.gpsimd.memset(zeros[:], 0.0)
            nc.gpsimd.memset(xls[:], 0.0)
            nc.gpsimd.memset(attblk[:], 0.0).then_inc(pre_ones, 1)
            nc.gpsimd.iota(iota_k_i, [[1, KI]], base=0, channel_multiplier=0)
            nc.gpsimd.iota(ki[:, 1, 0:CB], [[CS, CB]], base=0, channel_multiplier=1)
            nc.gpsimd.iota(ki[:, 2, 0:NB], [[BS, NB]], base=0, channel_multiplier=1).then_inc(pre_iota, 1)
            pool.wait_ge(pre_v, PV_COL)
            for b in range(NB):
                for to, frm in ((g_dst, dst), (g_src, src)):
                    nc.gpsimd.indirect_dma_start(
                        out=to[:, b, :], out_offset=None, in_=frm,
                        in_offset=bass.IndirectOffsetOnAxis(ap=ki[0:BS, 0, b:b + 1], axis=0)).then_inc(pre_gather, 16)

            def carry_wait():
                nc.gpsimd.tensor_tensor(pool_pad[:], zeros[:, 0:1], zeros[:, 0:1], ALU.add)

            def node_pool(l):
                cols = slice(D, ROW) if l == 2 else slice(0, ROW)

                def body(t, b):
                    T = t + l * TILES
                    pool.wait_ge(xls_ready, T + 1)
                    pool.dma_start(tab[l][bass.ds(t * P, P), :], xls[:, b, :]).then_inc(stored[b], 16)
                    if l == 2:
                        pool.wait_ge(h_ready, t + (TILES + 1))
                        pool.dma_start(hx_dram[bass.ds(t * P, P), :], hbuf[:, b, :]).then_inc(hx_stored[b], 16)
                    if l < 2:
                        pool.wait_ge(self_ready, T + 1)
                    else:
                        pool.wait_ge(xr_ready, T + 1)
                    part = [x3[:, bass.ds(t, 1), s, cols].rearrange("p o r -> p (o r)") for s in range(3)]
                    nc.gpsimd.tensor_copy(part[0], xr[:, b, cols]).then_inc(split_step, 1)
                    pool.wait_ge(split_step, T * 3 + 1)
                    carry_wait()
                    nc.gpsimd.tensor_tensor(r1[:, cols], xr[:, b, cols], part[0], ALU.subtract).then_inc(split_step, 1)
                    pool.wait_ge(split_step, T * 3 + 2)
                    nc.gpsimd.tensor_copy(part[1], r1[:, cols]).then_inc(split_step, 1)
                    pool.wait_ge(split_step, T * 3 + 3)
                    carry_wait()
                    nc.gpsimd.tensor_tensor(part[2], r1[:, cols], part[1], ALU.subtract).then_inc(split_done, 1)
                tiles(pool, body)
                pool.wait_ge(mm_done, (l + 1) * TILES)
                pool.wait_ge(split_done, (l + 1) * TILES)
                if l > 0:
                    pool.wait_ge(acc_read, l * TILES)
                if l == 2:
                    for b in range(2):
                        pool.wait_ge(hx_stored[b], 16 * ((TILES + 1 - b) // 2))
                for b in range(2):
                    pool.wait_ge(stored[b], 16 * ((TILES + 1 - b) // 2) * (l + 1))

            def gathers(l):
                def body(gh, b, fresh):
                    G1 = gh * 2 + (b + l * NG)
                    k0 = (gh * 2 + b) * GI
                    if not fresh:
                        pool.wait_ge(seg_done, G1 * GI - GI)
                    nc.gpsimd.tensor_copy(idx[:, b, :], src_items[:, bass.ds(k0, GI)]).then_inc(idx_ready, 1)
                    pool.wait_ge(idx_ready, G1 + 1)
                    carry_wait()
                    for i in range(GI):
                        nc.gpsimd.indirect_dma_start(
                            out=G[:, b, i, :], out_offset=None, in_=tab[l],
                            in_offset=bass.IndirectOffsetOnAxis(ap=idx[:, b, i:i + 1], axis=0)).then_inc(landed[b][i], 16)
                body(0, 0, l == 0)
                body(0, 1, l == 0)
                with pool.Fori(1, NG // 2) as j:
                    body(j, 0, False)
                    body(j, 1, False)

            for l in range(3):
                node_pool(l)
                if l == 0:
                    pool.wait_ge(pre_v, PV_END)
                gathers(l)

            def body(t, b):
                pool.wait_ge(h_ready, t + (2 * TILES + 1))
                pool.dma_start(out[bass.ds(t * P, P), :], hbuf[:, b, :]).then_inc(out_stored[b], 16)
            with pool.Fori(0, TILES // 2) as j:
                body(j * 2, 0)
                body(j * 2 + 1, 1)
            last = TILES - 1
            if TILES % 2:
                pool.wait_ge(h_ready, 3 * TILES)
                pool.dma_start(out[last * P:N, :], hbuf[0:LAST, 0, :]).then_inc(out_stored[0], 16)
            for b in range(2):
                pool.wait_ge(out_stored[b], 16 * ((TILES + 1 - b) // 2))

        @block.scalar
        def _(act):
            act.wait_ge(pre_pe, 2)
            for b in range(NB):
                ins = nc.scalar.activation(t_row[0:1, b * BS:(b + 1) * BS], pX[0:1, b // FB, (b % FB) * BS:(b % FB + 1) * BS], ACT.Copy)
            ins.then_inc(pre_act, 1)
            act.wait_ge(pre_pe, 3)
            for b in range(NB):
                ins = nc.scalar.activation(rel_items[:, b * BS:(b + 1) * BS], pZ[:, b // FB, (b % FB) * BS:(b % FB + 1) * BS], ACT.Copy)
            ins.then_inc(pre_act, 1)
            act.wait_ge(pre_pe, 4)
            for b in range(NB):
                ins = nc.scalar.activation(src_items[:, b * BS:(b + 1) * BS], pS[:, b // FB, (b % FB) * BS:(b % FB + 1) * BS], ACT.Copy)
            ins.then_inc(pre_act, 1)
            act.wait_ge(pre_pe, 5)
            for b in range(NB):
                at_b = slice((b % FB) * BS, (b % FB + 1) * BS)
                ins = nc.scalar.activation(last_items[:, b * BS:(b + 1) * BS], pS[:, b // FB, at_b], ACT.Copy)
            ins.then_inc(pre_act, 1)

            def node_act(l):
                def body(t, b):
                    T = t + l * TILES
                    if l == 1:
                        act.wait_ge(elu_in, t + 1)
                        nc.scalar.activation(ex, zs, ACT.Exp).then_inc(elu_exp, 1)
                    if l >= 2:
                        act.wait_ge(var_ready, t + ((l - 2) * TILES + 1))
                        nc.scalar.activation(small[:, 7, 2:3], small[:, 7, 1:2], ACT.Sqrt).then_inc(std_ready, 1)
                    if l == 3:
                        return
                    act.wait_ge(h_turned, T + 1)
                    nc.scalar.activation(hT[:, b, :], pZ[:, b, 0:D], ACT.Copy).then_inc(ht_ready, 1)
                    act.wait_ge(mm_done, T + 1)
                    width = ROW if l == 2 else D + 4
                    store_wait(t, b, l)
                    split_wait(t, b, l)
                    nc.scalar.activation(xls[:, b, 0:width], pX[:, b, 0:width], ACT.Copy).then_inc(xls_ready, 1)
                    if l < 2:
                        nc.scalar.activation(xr[:, b, 0:D + 4], pS[:, b, 0:D + 4], ACT.Copy).then_inc(xr_ready, 1)
                    else:
                        nc.scalar.activation(xr[:, b, D:ROW], pX[:, b, ROW:ROW + 8], ACT.Copy).then_inc(xr_ready, 1)

                def store_wait(t, b, l):
                    if l == 0 and static(t) and t < 2:
                        return
                    before = l * ((TILES + 1 - b) // 2)
                    half = (t - b) // 2 if static(t) else half_of[0]
                    act.wait_ge(stored[b], (half + before) * 16)

                def split_wait(t, b, l):
                    if l == 0 and static(t) and t < 2:
                        return
                    act.wait_ge(split_done, t + (l * TILES - 1))

                half_of = [None]
                body(0, 0)
                body(1, 1)
                with act.Fori(1, TILES // 2) as j:
                    half_of[0] = j
                    body(j * 2, 0)
                    body(j * 2 + 1, 1)
                if TILES % 2:
                    body(TILES - 1, 0)

            def edge_act(l):
                H = heads(l)

                def body(gh, b, first, second):
                    G1 = gh * 2 + (b + l * NG)
                    Gq = G1 - 1
                    q0 = (gh * 2 + b) * GI - GI
                    c = 1 - b

                    def relu(i):
                        act.wait_ge(zt_done, G1 * GI + (i + 1))
                        if not (static(G1) and G1 == 0 and i < 2):
                            act.wait_ge(log_done, G1 * GI + (i - 1))
                        nc.scalar.activation(reluT[:, i % 2, :], pZ[:, i % 2, 0:D], ACT.Relu).then_inc(relu_done, 1)

                    for i in range(GI):
                        if first and l < 2:
                            act.wait_ge(z_done, G1 * GI + (i + 1))
                            nc.scalar.activation(exs[:, b, i, :], pX[:, i % 2, D:ROW], ACT.Copy).then_inc(exs_done, 1)
                            if i >= 1:
                                relu(i - 1)
                        if second and i == 2:
                            rows_of = arow[0:1, :, 0:H * (GI + 1)].rearrange("o r (h k) -> o r h k", h=H)
                            act.wait_ge(s_ab, Gq + 1)
                            ends = pM[0:1, :].rearrange("o (r n) -> o r n", r=4)[:, :, 0:GI * H].rearrange("o r (h k) -> o r h k", h=H)
                            for r in range(2):
                                nc.scalar.activation(rows_of[:, r, :, 1:GI + 1], ends[:, r], ACT.Copy)
                            for r in range(2, 4):
                                ins = nc.scalar.activation(rows_of[:, r, :, 0:GI], ends[:, r], ACT.Copy)
                            ins.then_inc(s_arow, 1)
                        if second and i == 5:
                            act.wait_ge(s_d, Gq + 1)
                            nc.scalar.activation(fr[0:1, 2, 0:H], fr[0:1, 1, 0:H], ACT.Exp).then_inc(s_fx, 1)
                            nc.scalar.activation(G[:, c, :, D:D + H], per_h(dif, H), ACT.Exp).then_inc(s_w, 1)
                            if l < 2:
                                nc.scalar.activation(dself[:, 0:GI * H], dself[:, 0:GI * H], ACT.Exp).then_inc(s_ws, 1)
                    if first and l < 2:
                        relu(GI - 1)
                groups(act, l, body)

            for l in range(3):
                node_act(l)
                edge_act(l)
            node_act(3)

        @block.tensor
        def _(pe):
            pe.wait_ge(pre_v, PV_CMP)
            pe.wait_ge(pre_ones, 1)
            for b in range(NB):
                for j in range(CB):
                    mm = nc.tensor.matmul(pM[0:BS, b:b + 1], cmp[:, j, b * BS:(b + 1) * BS], ones_b[0:CS, 0:1],
                                          start=(j == 0), stop=(j == CB - 1))
            mm.then_inc(pre_pe, 1)
            pe.wait_ge(pre_v, PV_COL)

            def row_turn(bank, colf):
                for b in range(NB):
                    mm = nc.tensor.transpose(bank[0:1, b // FB, (b % FB) * BS:(b % FB + 1) * BS], colf(b), ident[0:BS, 0:BS])
                return mm

            def block_turn(bank, tile):
                for b in range(NB):
                    mm = nc.tensor.transpose(bank[:, b // FB, (b % FB) * BS:(b % FB + 1) * BS], tile[:, b, :], ident[0:BS, 0:BS])
                return mm

            row_turn(pX, lambda b: kf[0:BS, b:b + 1]).then_inc(pre_pe, 1)
            pe.wait_ge(pre_v, PV_REL)
            block_turn(pZ, rel).then_inc(pre_pe, 1)
            block_turn(pS, srcf).then_inc(pre_pe, 1)
            pe.wait_ge(pre_v, PV_FLAG)
            pe.wait_ge(pre_act, 3)
            block_turn(pS, lastf).then_inc(pre_pe, 1)
            pe.wait_ge(pre_act, 4)

            def node_pe(l):
                pe.wait_ge(w_ready, l + 1)

                def body(t, b, fresh):
                    T = t + l * TILES
                    if l == 0:
                        half = 0 if static(t) and t < 2 else (TILES // 2 if static(t) else None)
                        pe.wait_ge(h_in[b], (half_of[0] + 1) * 16)
                    else:
                        pe.wait_ge(h_ready, t + ((l - 1) * TILES + 1))
                    if not (l == 0 and fresh):
                        pe.wait_ge(ht_ready, T - 1)
                    for q in range(2):
                        mm = nc.tensor.transpose(pZ[:, b, q * P:(q + 1) * P], hbuf[:, b, q * P:(q + 1) * P], ident[:])
                    mm.then_inc(h_turned, 1)
                    pe.wait_ge(ht_ready, T + 1)
                    if not (l == 0 and fresh):
                        pe.wait_ge(xr_ready, T - 1)
                    A = (0, 272) if l == 2 else (0, D + 4)
                    for q in range(2):
                        mm = nc.tensor.matmul(pX[:, b, 0:A[1]], hT[:, b, q * P:(q + 1) * P], W[:, q, A[0]:A[1]],
                                              start=(q == 0), stop=(q == 1))
                    if l < 2:
                        for q in range(2):
                            mm = nc.tensor.matmul(pS[:, b, 0:D + 4], hT[:, b, q * P:(q + 1) * P], W[:, q, D + 4:2 * D + 8],
                                                  start=(q == 0), stop=(q == 1))
                    mm.then_inc(mm_done, 1)

                half_of = [0]
                body(0, 0, True)
                body(1, 1, True)
                with pe.Fori(1, TILES // 2) as j:
                    half_of[0] = j
                    body(j * 2, 0, False)
                    body(j * 2 + 1, 1, False)
                if TILES % 2:
                    half_of[0] = TILES // 2
                    body(TILES - 1, 0, False)

            def edge_pe(l):
                H = heads(l)
                pe.wait_ge(split_done, (l + 1) * TILES)
                pe.wait_ge(xr_ready, (l + 1) * TILES)
                if l < 2:
                    pe.wait_ge(s_wl, l + 1)

                def body(gh, b, first, second):
                    G1 = gh * 2 + (b + l * NG)
                    Gq = G1 - 1
                    k0 = (gh * 2 + b) * GI
                    c = 1 - b
                    if first:
                        _, tk = nc.values_load_multi_w_load_instructions(
                            t_row[0:1, bass.ds(k0, GI)], engines=(PE,), min_val=0, max_val=TILES - 1,
                            skip_runtime_bounds_check_because="t_k is a tile number by construction")
                        pe.wait_ge(dt_ready, G1 + 1)

                    def expand(i):
                        if l < 2:
                            if not (static(G1) and G1 == 0 and i < 2):
                                pe.wait_ge(z_done, G1 * GI + (i - 1))
                                pe.wait_ge(exs_done, G1 * GI + (i - 1))
                            to, cols = pX[:, i % 2, 0:ROW], slice(0, ROW)
                        else:
                            to, cols = pX[:, b, i * H:(i + 1) * H], slice(D, ROW)
                        for s in range(3):
                            mm = nc.tensor.matmul(to, DT[:, b, i * P:(i + 1) * P],
                                                  x3[:, bass.ds(tk[i], 1), s, cols].rearrange("p o r -> p (o r)"),
                                                  start=(s == 0), stop=(s == 2))
                        mm.then_inc(x_done, 1)

                    def turn(i):
                        pe.wait_ge(z_done, G1 * GI + (i + 1))
                        if not (static(G1) and G1 == 0 and i < 2):
                            pe.wait_ge(relu_done, G1 * GI + (i - 1))
                        for q in range(2):
                            mm = nc.tensor.transpose(pZ[:, i % 2, q * P:(q + 1) * P], Z[:, i % 2, q * P:(q + 1) * P], ident[:])
                        mm.then_inc(zt_done, 1)

                    def score(i):
                        pe.wait_ge(relu_done, G1 * GI + (i + 1))
                        for q in range(2):
                            mm = nc.tensor.matmul(pL[:, i * H:(i + 1) * H], reluT[:, i % 2, q * P:(q + 1) * P],
                                                  attblk[:, q, :], start=(q == 0), stop=(q == 1))
                        mm.then_inc(log_done, 1)

                    if first and l < 2:
                        expand(0)
                    for i in range(GI):
                        if first:
                            if l == 2:
                                expand(i)
                            elif i + 1 < GI:
                                expand(i + 1)
                        if second:
                            if i == 1:
                                pe.wait_ge(s_cand, Gq + 1)
                                nc.tensor.transpose(pM[:, 0:P], cand[:], ident[:]).then_inc(s_lt, 1)
                            if i == 2:
                                pe.wait_ge(s_scan, Gq + 1)
                                nc.tensor.transpose(pM[0:1, 0:P], flags[:, c, 2, P - 1:P], ident[:])
                                nc.tensor.transpose(pM[0:1, P:2 * P], F1[:, P - 1:P], ident[:])
                                nc.tensor.transpose(pM[0:1, 2 * P:3 * P], flags[:, c, 3, 0:1], ident[:])
                                nc.tensor.transpose(pM[0:1, 3 * P:4 * P], B1[:, 0:1], ident[:]).then_inc(s_ab, 1)
                            if i == 3:
                                pe.wait_ge(s_cin, Gq + 1)
                                nc.tensor.matmul(pM[:, 0:1], carry_in[0:1, 0, :], ones[0:1, 0:1], start=True, stop=True)
                                nc.tensor.matmul(pM[:, 1:2], carry_in[0:1, 1, :], ones[0:1, 0:1], start=True, stop=True).then_inc(s_carc, 1)
                            if i == 4:
                                pe.wait_ge(s_m, Gq + 1)
                                nc.tensor.transpose(pM[:, 3 * P:4 * P], mT[:], ident[:]).then_inc(s_me, 1)
                            if i == 6:
                                pe.wait_ge(s_fx, Gq + 1)
                                nc.tensor.matmul(pM[:, 8:8 + H], ones[0:1, :], fr[0:1, 2, 0:H], start=True, stop=True).then_inc(s_fb, 1)
                            for n in SECOND.get(i, ()):
                                pe.wait_ge(wg_done, Gq * GI + (n + 1))
                                if not (static(Gq) and Gq == 0 and n < 2):
                                    pe.wait_ge(acc_done, Gq * GI + (n - 1))
                                nc.tensor.matmul(pS[:, n % 2, 0:ROW], Dm[:, n % 4, :], G[:, c, n, :], start=True, stop=True).then_inc(seg_done, 1)
                        if first and l < 2:
                            if i >= 1:
                                turn(i - 1)
                            if i >= 2:
                                score(i - 2)
                    if first and l < 2:
                        turn(GI - 1)
                        score(GI - 2)
                        score(GI - 1)
                groups(pe, l, body)

            for l in range(3):
                node_pe(l)
                edge_pe(l)

        @block.vector
        def _(dve):
            v = nc.vector
            n_pre = [0]

            def pre(ins, mark=None):
                n_pre[0] += 1
                ins.then_inc(pre_v, 1)
                dve.wait_ge(pre_v, n_pre[0])
                assert mark is None or mark == n_pre[0], (mark, n_pre[0])

            dve.wait_ge(pre_iota, 1)
            pre(v.tensor_copy(kbig, iota_k_i))
            pre(v.tensor_copy(iota_row[:], kbig[:, 0:P]))
            dve.wait_ge(pre_ld, 16)
            pre(v.tensor_single_scalar(ki[0:CS, 0, 0:CB], ki[0:CS, 0, 0:CB], 7, ALU.arith_shift_right))
            pre(v.tensor_copy(kf[0:CS, 0:CB], ki[0:CS, 0, 0:CB]))
            pre(v.tensor_copy(cols[0:CS, 0:CB], ki[0:CS, 1, 0:CB]))
            pre(v.tensor_tensor(kf[0:CS, 0:CB], kf[0:CS, 0:CB], cols[0:CS, 0:CB], ALU.add))
            for j in range(CB):
                ins = v.tensor_scalar(cmp[:, j, :], kbig[0:CS, 0:ITEMS], kf[0:CS, j:j + 1], None, ALU.is_gt)
            pre(ins, PV_CMP)
            pre(v.tensor_copy(iota_part[:], ki[:, 2, 0:1]))
            pre(v.tensor_scalar(ident[:], iota_row[:], iota_part[:, 0:1], None, ALU.is_equal))
            dve.wait_ge(pre_pe, 1)
            pre(v.tensor_copy(ki[0:BS, 0, 0:NB], pM[0:BS, 0:NB]))
            pre(v.tensor_copy(kf[0:BS, 0:NB], ki[0:BS, 2, 0:NB]))
            pre(v.tensor_tensor(kf[0:BS, 0:NB], kf[0:BS, 0:NB], pM[0:BS, 0:NB], ALU.subtract), PV_COL)
            tcol = cols[0:BS, 0:NB]
            pre(v.tensor_scalar(tcol, kf[0:BS, 0:NB], float(P), None, ALU.mult))
            dve.wait_ge(pre_gather, 32 * NB)
            pre(v.tensor_copy(dstf, g_dst))
            pre(v.tensor_copy(srcf, g_src))
            pre(v.tensor_tensor(rel, dstf, tcol.unsqueeze(2).to_broadcast([BS, NB, P]), ALU.subtract))
            pre(v.tensor_scalar(nxt, rel, 0.0, None, ALU.is_ge))
            pre(v.tensor_scalar(key, rel, float(P), None, ALU.is_lt))
            pre(v.tensor_tensor(nxt, nxt, key, ALU.mult))
            pre(v.scalar_tensor_tensor(rel, rel, 1.0, nxt, ALU.add, ALU.mult))
            pre(v.tensor_scalar(rel, rel, -1.0, None, ALU.add))
            pre(v.tensor_copy(relbf, rel))
            pre(v.scalar_tensor_tensor(key, dstf, 1.0, nxt, ALU.add, ALU.mult), PV_REL)
            dve.wait_ge(pre_shift, 32)
            for f, other in ((0, prev), (1, nxt)):
                pre(v.tensor_tensor(dstf, key, other, ALU.is_equal))
                pre(v.tensor_scalar(flg[:, :, f, :], dstf, -1.0, BIG, ALU.add, ALU.mult))
            pre(v.tensor_scalar(lastf, flg[:, :, 1, :], -1.0, None, ALU.is_lt))
            for b in range(NB):
                v.tensor_tensor_scan(flg[:, b, 2, :], flg[:, b, 0, :], flg[:, b, 0, :], 0.0, ALU.min, ALU.min)
                ins = v.tensor_tensor_scan(flg[:, b, 3, ::-1], flg[:, b, 1, ::-1], flg[:, b, 1, ::-1], 0.0, ALU.min, ALU.min)
            pre(ins, PV_FLAG)
            dve.wait_ge(pre_flag, 16)
            dve.wait_ge(pre_rel, 16)
            dve.wait_ge(pre_act, 4)
            pre(v.memset(acc_mem[:, 0:TILES * ROW], 0.0))
            for a in (cand, F1, B1, mT, carry_in, flags):
                v.memset(a[:], 0.0)
            pre(v.memset(arow[:], -BIG), PV_END)

            n_w = [0]

            def wlink(ins):
                n_w[0] += 1
                ins.then_inc(wchain, 1)
                dve.wait_ge(wchain, n_w[0])

            def prepare_weights(l):
                dve.wait_ge(w_in, W_IN[l])
                H = heads(l)
                C = D // H
                for q in range(2):
                    for s in range(2):
                        w = W[:, q, 0:D] if (l == 2 or s == 0) else W[:, q, D + 4:2 * D + 4]
                        o = (D + 8 * s) if l == 2 else (D if s == 0 else 2 * D + 4)
                        wlink(v.tensor_tensor(wtmp, w, attb[:, s if l == 2 else 0, :], ALU.mult))
                        wlink(v.tensor_reduce(W[:, q, o:o + H], wtmp.rearrange("p (h c) -> p h c", h=H), AX.X, ALU.add))
                        if l < 2:
                            wlink(v.tensor_scalar(W[:, q, o:o + H], W[:, q, o:o + H], SLOPE, None, ALU.mult))
                v.tensor_copy(r1w[:], attb[:, 0, 0:1]).then_inc(w_ready, 1)

            r1w = onehot0[:, 0:1]

            def node_dve(l):
                PER = NODE_STEPS[l]
                base = sum(NODE_STEPS[:l]) * TILES
                H = heads(l - 1)

                def body(t, b, fresh):
                    n = [0]

                    def link(ins):
                        n[0] += 1
                        ins.then_inc(node_step, 1)
                        dve.wait_ge(node_step, t * PER + (base + n[0]))

                    T = t + l * TILES
                    if not (static(t) and t == 0):
                        if l < 2:
                            dve.wait_ge(self_ready, T)
                        else:
                            dve.wait_ge(acc_read, t + (l - 1) * TILES)
                    if l > 0:
                        a = acc[:, bass.ds(t, 1), :].rearrange("p o r -> p (o r)")
                        num, den, ws = a[:, 0:D], a[:, D:D + H], a[:, D + 4:D + 8]
                        den1, e0, wsx, den2, rd = (small[:, s, 0:H] for s in range(5))

                        def bc(ap):
                            return ap.unsqueeze(2).to_broadcast([P, H, D // H])

                        def hv(ap):
                            return ap.rearrange("p (h c) -> p h c", h=H)
                        if l < 3:
                            dve.wait_ge(own_in[b], (half_of[0] + (1 if l == 1 else 1 + (TILES + 1 - b) // 2)) * 16)
                        if l < 3:
                            link(v.tensor_tensor(den1, den, ws, ALU.add))
                            link(v.tensor_scalar(e0, den1, 0.0, None, ALU.is_equal))
                            link(v.tensor_tensor(wsx, ws, e0, ALU.add))
                            link(v.scalar_tensor_tensor(den2, den1, 1e-16, e0, ALU.add, ALU.add))
                        else:
                            link(v.tensor_scalar(e0, den, 0.0, None, ALU.is_equal))
                            link(v.tensor_tensor(den2, den, e0, ALU.add))
                        link(v.reciprocal(rd, den2))
                        if l < 3:
                            link(v.tensor_tensor(hv(tmp), hv(own[:, b, 0:D]), bc(wsx), ALU.mult))
                            link(v.tensor_tensor(tmp, tmp, num, ALU.add))
                            link(v.tensor_tensor(hv(tmp), hv(tmp), bc(rd), ALU.mult))
                            link(v.tensor_tensor(tmp, tmp, bias, ALU.add))
                        else:
                            link(v.tensor_tensor(hv(tmp), hv(num), bc(rd), ALU.mult))
                        if l == 1:
                            v.tensor_scalar(zs, tmp, 0.0, None, ALU.min).then_inc(elu_in, 1)
                            link(v.tensor_scalar(tmp, tmp, 0.0, None, ALU.max))
                            dve.wait_ge(elu_exp, t + 1)
                            if not fresh:
                                dve.wait_ge(h_turned, T - 1)
                            v.scalar_tensor_tensor(hbuf[:, b, :], ex, -1.0, tmp, ALU.add, ALU.add).then_inc(h_ready, 1)
                        else:
                            dve.wait_ge(res_in[b], (half_of[0] + (1 if l == 2 else 1 + (TILES + 1 - b) // 2)) * 16)
                            link(v.tensor_tensor(tmp, tmp, res[:, b, :], ALU.add))
                            link(v.bn_stats(small[:, 5, 0:6], tmp))
                            v.memset(small[:, 4, 7:8], 0.0)
                            link(v.bn_aggr(small[:, 6, 0:2], small[:, 5, 0:6]))
                            v.tensor_scalar(small[:, 7, 1:2], small[:, 6, 1:2], EPS, None, ALU.add).then_inc(var_ready, 1)
                            dve.wait_ge(std_ready, t + ((l - 2) * TILES + 1))
                            link(v.reciprocal(small[:, 7, 0:1], small[:, 7, 2:3]))
                            if not fresh:
                                if l == 2:
                                    dve.wait_ge(h_turned, T - 1)
                                    dve.wait_ge(hx_stored[b], half_of[0] * 16)
                                else:
                                    dve.wait_ge(out_stored[b], half_of[0] * 16)
                            v.tensor_scalar(hbuf[:, b, :], tmp, small[:, 6, 0:1], small[:, 7, 0:1], ALU.subtract, ALU.mult).then_inc(h_ready, 1)
                        if l < 3:
                            v.tensor_copy(a, zeros[:]).then_inc(acc_read, 1)
                        else:
                            v.memset(small[:, 0, 0:1], 0.0).then_inc(acc_read, 1)
                    if l < 2:
                        dve.wait_ge(xls_ready, T + 1)
                        dve.wait_ge(xr_ready, T + 1)
                        link(v.tensor_tensor(zs, xls[:, b, 0:D], xr[:, b, 0:D], ALU.add))
                        link(v.scalar_tensor_tensor(zs, zs, SLOPE, zs, ALU.mult, ALU.max))
                        link(v.tensor_tensor(zs, zs, attb[:, 0, :], ALU.mult))
                        v.tensor_reduce(xr[:, b, D + 4:ROW], zs.rearrange("p (h c) -> p h c", h=4), AX.X, ALU.add).then_inc(self_ready, 1)
                    assert n[0] == PER, (l, n[0])

                half_of = [0]
                body(0, 0, True)
                body(1, 1, True)
                with dve.Fori(1, TILES // 2) as j:
                    half_of[0] = j
                    body(j * 2, 0, False)
                    body(j * 2 + 1, 1, False)
                if TILES % 2:
                    half_of[0] = TILES // 2
                    body(TILES - 1, 0, False)

            def edge_dve(l):
                H = heads(l)
                HG = H * GI
                RW = H * (GI + 1)
                if l < 2:
                    dve.wait_ge(att_in, 64 * (l + 1))
                    v.tensor_scalar(attblk[:], attblk[:], 1.0 - SLOPE, None, ALU.mult).then_inc(s_wl, 1)
                rows_of = arow[0:1, :, 0:RW].rearrange("o r (h k) -> o r h k", h=H)
                if l > 0:
                    v.memset(arow[:], -BIG).then_inc(pre_acc, 1)
                    dve.wait_ge(pre_acc, l)

                def spread(gh, b):
                    dve.wait_ge(relb_in[b], landed_need(l, gh))
                    v.tensor_scalar(DT[:, b, :], DT[:, b, :], iota_part[:, 0:1], None, ALU.is_equal).then_inc(dt_ready, 1)

                spread(0, 0)

                def body(gh, b, first, second):
                    G1 = gh * 2 + (b + l * NG)
                    Gq = G1 - 1
                    c = 1 - b
                    q0 = (gh * 2 + b) * GI - GI
                    qh = gh if b == 1 else gh - 1
                    last_group = static(gh) and gh == NG // 2 - 1 and b == 1
                    if second:
                        _, tq = nc.values_load_multi_w_load_instructions(
                            t_row[0:1, bass.ds(q0, GI)], engines=(DVE,), min_val=0, max_val=TILES - 1,
                            skip_runtime_bounds_check_because="t_k is a tile number by construction")

                    def acc_at(n):
                        return acc[:, bass.ds(tq[n], 1), :].rearrange("p o r -> p (o r)")

                    def add(n):
                        dve.wait_ge(seg_done, Gq * GI + (n + 1))
                        if n > 0:
                            dve.wait_ge(acc_done, Gq * GI + n)
                        v.tensor_tensor(acc_at(n), acc_at(n), pS[:, n % 2, 0:ROW], ALU.add).then_inc(acc_done, 1)

                    for i in range(GI):
                        if first and l < 2:
                            dve.wait_ge(landed[b][i], landed_need(l, gh))
                            dve.wait_ge(x_done, G1 * GI + (i + 1))
                            if not (static(G1) and G1 == 0 and i < 2):
                                dve.wait_ge(zt_done, G1 * GI + (i - 1))
                            v.tensor_tensor(Z[:, i % 2, :], G[:, b, i, 0:D], pX[:, i % 2, 0:D], ALU.add).then_inc(z_done, 1)
                        if second:
                            if i == 1:
                                pl = (pL[:, 0:HG] if l < 2 else pX[:, c, 0:HG]).rearrange("p (i h) -> p i h", h=H)
                                if l < 2:
                                    dve.wait_ge(log_done, Gq * GI + GI)
                                    dve.wait_ge(exs_done, Gq * GI + GI)
                                    v.tensor_tensor(per_h(lr, H), pl, G[:, c, :, D:D + 4], ALU.add).then_inc(s_l1, 1)
                                    dve.wait_ge(s_l1, Gq + 1)
                                    v.tensor_tensor(per_h(lr, H), per_h(lr, H), exs[:, c, :, 0:4], ALU.add).then_inc(s_l2, 1)
                                    dve.wait_ge(s_l2, Gq + 1)
                                    v.tensor_tensor(per_h(cand, H), per_h(lr, H), exs[:, c, :, 4:8], ALU.max).then_inc(s_cand, 1)
                                else:
                                    dve.wait_ge(x_done, Gq * GI + GI)
                                    for n in range(GI):
                                        dve.wait_ge(landed[c][n], landed_need(l, qh))
                                    v.tensor_tensor(per_h(lr, H), pl, G[:, c, :, D:ROW], ALU.add).then_inc(s_l1, 1)
                                    dve.wait_ge(s_l1, Gq + 1)
                                    v.scalar_tensor_tensor(cand[:, 0:HG], lr[:, 0:HG], SLOPE, lr[:, 0:HG], ALU.mult, ALU.max).then_inc(s_cand, 1)
                            if i == 2:
                                dve.wait_ge(s_lt, Gq + 1)
                                dve.wait_ge(*flags_need(l, qh, c))
                                v.tensor_tensor_scan(F1[0:HG, :], flags[0:HG, c, 0, :], pM[0:HG, 0:P], -BIG, ALU.add, ALU.max)
                                v.tensor_tensor_scan(B1[0:HG, ::-1], flags[0:HG, c, 1, ::-1], pM[0:HG, 0:P][:, ::-1], -BIG, ALU.add, ALU.max).then_inc(s_scan, 1)
                            if i == 3:
                                dve.wait_ge(s_arow, Gq + 1)
                                v.tensor_tensor_scan(Fout[0:1, 0:RW], arow[0:1, 0, 0:RW], arow[0:1, 1, 0:RW], -BIG, ALU.add, ALU.max)
                                v.tensor_tensor_scan(Bout[0:1, 0:RW][:, ::-1], arow[0:1, 2, 0:RW][:, ::-1], arow[0:1, 3, 0:RW][:, ::-1],
                                                     -BIG, ALU.add, ALU.max).then_inc(s_car, 1)
                                dve.wait_ge(s_car, Gq + 1)
                                v.tensor_copy(carry_in[0:1, 0, 0:HG].rearrange("o (h k) -> o h k", h=H),
                                              Fout[0:1, 0:RW].rearrange("o (h k) -> o h k", h=H)[:, :, 0:GI])
                                v.tensor_copy(carry_in[0:1, 1, 0:HG].rearrange("o (h k) -> o h k", h=H),
                                              Bout[0:1, 0:RW].rearrange("o (h k) -> o h k", h=H)[:, :, 1:GI + 1]).then_inc(s_cin, 1)
                            if i == 4:
                                dve.wait_ge(s_carc, Gq + 1)
                                v.scalar_tensor_tensor(F1[0:HG, :], flags[0:HG, c, 2, :], pM[0:HG, 0:1], F1[0:HG, :], ALU.add, ALU.max)
                                v.scalar_tensor_tensor(B1[0:HG, :], flags[0:HG, c, 3, :], pM[0:HG, 1:2], B1[0:HG, :], ALU.add, ALU.max).then_inc(s_t, 1)
                                dve.wait_ge(s_t, Gq + 1)
                                v.tensor_tensor(mT[0:HG, :], F1[0:HG, :], B1[0:HG, :], ALU.max).then_inc(s_m, 1)
                            if i == 5:
                                dve.wait_ge(s_me, Gq + 1)
                                me = pM[:, 3 * P:3 * P + HG]
                                lo = lr if l < 2 else cand
                                v.tensor_tensor(fr[0:1, 0, 0:H], rows_of[:, 1, :, 0], me[0:1].rearrange("p (h i) -> p h i", h=H)[:, :, 0], ALU.subtract).then_inc(s_fr, 1)
                                v.tensor_tensor(dif[:, 0:HG], lo[:, 0:HG], me, ALU.subtract)
                                if l < 2:
                                    v.tensor_tensor(per_h(dself, H), exs[:, c, :, 4:8], me.rearrange("p (h i) -> p i h", h=H), ALU.subtract)
                                dve.wait_ge(s_fr, Gq + 1)
                                v.tensor_scalar(fr[0:1, 1, 0:H], fr[0:1, 0, 0:H], 0.0, None, ALU.min).then_inc(s_d, 1)
                            if i == 6:
                                v.tensor_copy(onehot0[:, 0:1], DT[:, c, 0:1]).then_inc(s_oh, 1)
                                dve.wait_ge(s_oh, Gq + 1)
                                v.tensor_scalar(onehot0[:, 1:2], onehot0[:, 0:1], -1.0, 1.0, ALU.mult, ALU.add).then_inc(s_noh, 1)
                                dve.wait_ge(s_noh, Gq + 1)
                                v.tensor_copy(rows_of[:, 1, :, 0], Fout[0:1, 0:RW].rearrange("o (h k) -> o h k", h=H)[:, :, GI]).then_inc(s_cp, 1)
                            if i == 7:
                                if l < 2:
                                    dve.wait_ge(s_ws, Gq + 1)
                                    dve.wait_ge(s_w, Gq + 1)
                                    v.tensor_tensor(G[:, c, :, D + 4:ROW], per_h(dself, H),
                                                    last_items[:, bass.ds(q0, GI)].unsqueeze(2).to_broadcast([P, GI, 4]), ALU.mult)
                                dve.wait_ge(s_fb, Gq + 1)
                                v.tensor_scalar(resc[:, 0:H], pM[:, 8:8 + H], onehot0[:, 0:1], onehot0[:, 1:2], ALU.mult, ALU.add).then_inc(s_sc, 1)
                                dve.wait_ge(s_sc, Gq + 1)
                                if not (static(Gq) and Gq == 0):
                                    dve.wait_ge(acc_done, Gq * GI)
                                a = acc_at(0)
                                ah = a[:, 0:D].rearrange("p (h d) -> p h d", h=H)
                                v.tensor_tensor(ah, ah, resc[:, 0:H].unsqueeze(2).to_broadcast([P, H, D // H]), ALU.mult)
                                v.tensor_tensor(a[:, D:D + H], a[:, D:D + H], resc[:, 0:H], ALU.mult).then_inc(s_resc, 1)
                                dve.wait_ge(s_resc, Gq + 1)
                                dve.wait_ge(s_w, Gq + 1)
                            for n in SECOND.get(i, ()):
                                if not (static(Gq) and Gq == 0 and n < 4):
                                    dve.wait_ge(seg_done, Gq * GI + (n - 3))
                                v.tensor_scalar(Dm[:, n % 4, :], iota_row[:], rel_items[:, bass.ds(q0 + n, 1)], None, ALU.is_equal)
                                gv = G[:, c, n, 0:D].rearrange("p (h d) -> p h d", h=H)
                                v.tensor_tensor(gv, gv, G[:, c, n, D:D + H].unsqueeze(2).to_broadcast([P, H, D // H]), ALU.mult).then_inc(wg_done, 1)
                                if n > 0:
                                    add(n - 1)
                        if i == 14 and first and not last_group:
                            spread(gh + b, 1 - b)
                    if second:
                        add(GI - 1)
                groups(dve, l, body)

            for l in range(3):
                prepare_weights(l)
                node_dve(l)
                edge_dve(l)
                dve.wait_ge(acc_done, (l + 1) * NG * GI)
            node_dve(3)


PV_CMP, PV_COL, PV_REL, PV_FLAG, PV_END = 7, 12, 23, 29, 31
W_IN = [48, 112, 192]
NODE_STEPS = [3, 13, 13, 8]


def kernel(**inputs):
    import numpy as np
    import concourse.bacc as bacc
    from concourse.bass_utils import run_bass_kernel_spmd

    x = np.asarray(inputs["x"])
    src, dst = np.asarray(inputs["src"]), np.asarray(inputs["dst"])
    n, e = x.shape[0], src.shape[0]
    tiles, chunks, _ = sizes(n, e)
    xp = np.zeros((tiles * P, D), x.dtype)
    xp[:n] = x
    srcp = np.zeros((chunks * P,), src.dtype)
    srcp[:e] = src
    dstp = np.full((chunks * P,), tiles * P - 1, dst.dtype)
    dstp[:e] = dst
    arrays = {"x": xp, "src": srcp.reshape(chunks, P), "dst": dstp.reshape(chunks, P)}
    for name in ("L0_gnn_Wl1", "L0_gnn_Wr1", "L0_gnn_att1", "L0_gnn_b1", "L0_gnn_Wl2", "L0_gnn_Wr2", "L0_gnn_att2",
                 "L0_gnn_b2", "L1_gnn_W", "L1_gnn_a"):
        arrays[name] = np.ascontiguousarray(inputs[name])
    nc = bacc.Bacc("TRN2", target_bir_lowering=False, num_devices=1)
    aps = [nc.dram_tensor(f"in_{k}", a.shape, mybir.dt.from_np(a.dtype), kind="ExternalInput").ap() for k, a in arrays.items()]
    out = nc.dram_tensor("out_0", (n, D), F32, kind="ExternalOutput").ap()
    gnn_program(nc, *aps, out)
    r = run_bass_kernel_spmd(nc, [{f"in_{k}": a for k, a in arrays.items()}], core_ids=[0])
    return r.results[0]["out_0"]
```

```python
from contextlib import ExitStack

import concourse.bass as bass
from concourse import mybir

P = 128
GI = 16
D = 256
ROW = D + 8
BIG = 1e30
SLOPE = 0.2
EPS = 1e-5

ALU = mybir.AluOpType
ACT = mybir.ActivationFunctionType
AX = mybir.AxisListType
F32 = mybir.dt.float32
BF16 = mybir.dt.bfloat16
I32 = mybir.dt.int32
DVE = mybir.EngineType.DVE
PE = mybir.EngineType.PE


def sizes(n_nodes, n_edges):
    tiles = -(-n_nodes // P)
    chunks = n_edges // P + 1
    while (chunks + tiles - 1) % (2 * GI):
        chunks += 1
    return tiles, chunks, chunks + tiles - 1


def cut(n):
    blocks = next(b for b in range(1, n + 1) if n % b == 0 and n // b <= P)
    return blocks, n // blocks


def gnn_program(nc, x, src, dst, wl1, wr1, att1, b1, wl2, wr2, att2, b2, w_gat, a_gat, out):
    N = out.shape[0]
    CHUNKS = dst.shape[0]
    TILES = x.shape[0] // P
    ITEMS = CHUNKS + TILES - 1
    NG = ITEMS // GI
    NB, BS = cut(ITEMS)
    CB, CS = cut(CHUNKS)
    assert NG % 2 == 0 and NG >= 6 and N % P and TILES >= 8
    FB = 4
    LAST = N - (TILES - 1) * P

    tab = [nc.dram_tensor(f"table{l}", (TILES * P, ROW), F32, kind="Internal").ap() for l in range(3)]
    hx_dram = nc.dram_tensor("hx_dram", (TILES * P, D), F32, kind="Internal").ap()
    rel_dram = nc.dram_tensor("rel_dram", (ITEMS, P), BF16, kind="Internal").ap()
    key_dram = nc.dram_tensor("key_dram", (ITEMS * P + 2,), F32, kind="Internal").ap()
    flag_dram = nc.dram_tensor("flag_dram", (ITEMS, 4 * P), F32, kind="Internal").ap()

    with ExitStack() as ctx:
        def sb(name, shape, dt=F32):
            return ctx.enter_context(nc.sbuf_tensor(name, shape, dt))

        def psum(name, shape):
            return ctx.enter_context(nc.psum_tensor(name, shape, F32))

        def sem(name):
            return ctx.enter_context(nc.semaphore(name))

        x3 = sb("x3", [P, TILES, 3, ROW], BF16)
        scratch_words = 23 * NB * P // 2 + max(ITEMS, P) + 3 * 64
        acc_mem = sb("acc_mem", [P, max(TILES * ROW, scratch_words)])
        acc = acc_mem[:, 0:TILES * ROW].rearrange("p (t r) -> p t r", r=ROW)
        G = sb("gathered", [P, 2, GI, ROW])
        src_items = sb("src_items", [P, ITEMS], I32)
        rel_items = sb("rel_items", [P, ITEMS])
        last_items = sb("last_items", [P, ITEMS], BF16)
        t_row = sb("t_row", [1, ITEMS], I32)
        ident = sb("ident", [P, P])
        iota_row = sb("iota_row", [P, P])
        iota_part = sb("iota_part", [P, 1])
        ones = sb("ones", [P, P])
        ones_b = sb("ones_b", [P, 1], BF16)
        zeros = sb("zeros", [P, ROW])
        idx = sb("idx", [P, 2, GI], I32)
        DT = sb("DT", [P, 2, GI * P], BF16)
        Dm = sb("Dm", [P, 4, P])
        Z = sb("Z", [P, 2, D])
        reluT = sb("reluT", [P, 2, D])
        exs = sb("exs", [P, 2, GI, 8])
        flags = sb("flags", [P, 2, 4, P])
        F1 = sb("F1", [P, P])
        B1 = sb("B1", [P, P])
        mT = sb("mT", [P, P])
        lr = sb("lr", [P, P])
        cand = sb("cand", [P, P])
        dif = sb("dif", [P, P])
        dself = sb("dself", [P, P])
        arow = sb("arow", [1, 4, 8 * (GI + 1)])
        Fout = sb("Fout", [1, 8 * (GI + 1)])
        Bout = sb("Bout", [1, 8 * (GI + 1)])
        carry_in = sb("carry_in", [1, 2, 8 * GI])
        fr = sb("fr", [1, 3, 8])
        onehot0 = sb("onehot0", [P, 2])
        resc = sb("resc", [P, 8])
        attpad = sb("attpad", [P, 2, 5 * GI - 1])
        g_at = [0]

        def in_g(*shape):
            words = 1
            for n in shape:
                words *= n
            a = G[:].rearrange("p b i r -> p (b i r)")[:, g_at[0]:g_at[0] + words]
            g_at[0] += words
            return a if len(shape) == 1 else a.rearrange("p (a c) -> p a c", a=shape[0])

        W = in_g(2, 544)
        attb = in_g(2, D)
        bias = in_g(D)
        wtmp = in_g(D)
        hbuf = in_g(2, D)
        hT = in_g(2, D)
        r1 = in_g(2, ROW)
        selfs = in_g(TILES, 4)
        zs = in_g(D)
        own = in_g(2, ROW)
        res = in_g(2, D)
        tmp = in_g(2, D)
        ex = in_g(2, D)
        pos = in_g(2, D)
        nd = in_g(4, 8 * TILES)
        xls = sb("xls", [P, 2, ROW])
        xr = sb("xr", [P, 2, ROW])
        small = sb("small", [P, 8, 8])
        pool_pad = sb("pool_pad", [P, 8])
        pX = psum("pX", [P, 2, 512])
        pZ = psum("pZ", [P, 2, 512])
        pS = psum("pS", [P, 2, 512])
        pL = psum("pL", [P, 512])
        pM = psum("pM", [P, 512])

        at = [0]

        def carve(words):
            a = acc_mem[:, at[0]:at[0] + words]
            at[0] += words
            assert at[0] <= acc_mem.shape[1]
            return a

        g_src = carve(NB * P).bitcast(I32)[0:BS].rearrange("p (b e) -> p b e", b=NB)
        g_dst = carve(NB * P).bitcast(I32)[0:BS].rearrange("p (b e) -> p b e", b=NB)
        dstf = carve(NB * P)[0:BS].rearrange("p (b e) -> p b e", b=NB)
        rel = carve(NB * P)[0:BS].rearrange("p (b e) -> p b e", b=NB)
        key = carve(NB * P)[0:BS].rearrange("p (b e) -> p b e", b=NB)
        prev = carve(NB * P)[0:BS].rearrange("p (b e) -> p b e", b=NB)
        nxt = carve(NB * P)[0:BS].rearrange("p (b e) -> p b e", b=NB)
        flg = carve(NB * 4 * P)[0:BS].rearrange("p (b f e) -> p b f e", b=NB, f=4)
        relbf = carve(NB * P // 2).bitcast(BF16)[0:BS].rearrange("p (b e) -> p b e", b=NB)
        srcf, lastf = prev, dstf
        KI = max(ITEMS, P)
        assert KI <= 8 * P
        iota_k_i = flags[:].rearrange("p b f e -> p (b f e)")[:, 0:KI].bitcast(I32)
        kbig = carve(KI)
        cols = carve(16 * 8)
        cmp = x3[:].rearrange("p t s r -> p (t s r)") if CB * ITEMS <= TILES * 3 * ROW else sb("cmp", [P, CB * ITEMS], BF16)[:]
        cmp = cmp[0:CS, 0:CB * ITEMS].rearrange("p (j k) -> p j k", j=CB)
        kf = carve(16)
        ki = carve(48).bitcast(I32).rearrange("p (a c) -> p a c", a=3)

        pre_ld = sem("pre_ld")
        pre_iota = sem("pre_iota")
        pre_ones = sem("pre_ones")
        pre_v = sem("pre_v")
        pre_pe = sem("pre_pe")
        pre_act = sem("pre_act")
        pre_gather = sem("pre_gather")
        pre_rel = sem("pre_rel")
        pre_key = sem("pre_key")
        pre_shift = sem("pre_shift")
        pre_flag = sem("pre_flag")
        pre_acc = sem("pre_acc")
        w_in = sem("w_in")
        att_in = sem("att_in")
        w_ready = sem("w_ready")
        wchain = sem("wchain")
        h_in = [sem(f"h_in{b}") for b in range(2)]
        own_in = [sem(f"own_in{b}") for b in range(2)]
        res_in = [sem(f"res_in{b}") for b in range(2)]
        h_ready = sem("h_ready")
        h_turned = sem("h_turned")
        ht_ready = sem("ht_ready")
        mm_done = sem("mm_done")
        xls_ready = sem("xls_ready")
        xr_ready = sem("xr_ready")
        self_ready = sem("self_ready")
        split_done = sem("split_done")
        rest_done = sem("rest_done")
        middle_done = sem("middle_done")
        self_split = sem("self_split")
        node_step = sem("node_step")
        o_ready = sem("o_ready")
        elu_neg = sem("elu_neg")
        rstd_ready = sem("rstd_ready")
        self_step = sem("self_step")
        den_step = sem("den_step")
        acc_zero = sem("acc_zero")
        elu_exp = sem("elu_exp")
        var_ready = sem("var_ready")
        std_ready = sem("std_ready")
        acc_read = sem("acc_read")
        stored = [sem(f"stored{b}") for b in range(2)]
        hx_stored = [sem(f"hx_stored{b}") for b in range(2)]
        out_stored = [sem(f"out_stored{b}") for b in range(2)]
        landed = [[sem(f"landed{b}_{i}") for i in range(GI)] for b in range(2)]
        x_done = sem("x_done")
        z_done = sem("z_done")
        exs_done = sem("exs_done")
        zt_done = sem("zt_done")
        relu_done = sem("relu_done")
        log_done = sem("log_done")
        wg_done = sem("wg_done")
        seg_done = sem("seg_done")
        acc_done = sem("acc_done")
        idx_ready = sem("idx_ready")
        relb_in = [sem(f"relb_in{b}") for b in range(2)]
        flags_in = [[sem(f"flags_in{h}_{b}") for b in range(2)] for h in (4, 8)]
        dt_ready = sem("dt_ready")
        s_l1, s_l2, s_cand, s_lt, s_scan, s_ab, s_arow, s_car, s_carc, s_t, s_m, s_me = (
            sem(n) for n in ("s_l1", "s_l2", "s_cand", "s_lt", "s_scan", "s_ab", "s_arow", "s_car",
                             "s_carc", "s_t", "s_m", "s_me"))
        s_fr, s_d, s_fx, s_w, s_ws, s_fb, s_wl, s_oh, s_noh, s_sc, s_resc, s_cp = (
            sem(n) for n in ("s_fr", "s_d", "s_fx", "s_w", "s_ws", "s_fb", "s_wl", "s_oh", "s_noh",
                             "s_sc", "s_resc", "s_cp"))

        s_cin = sem("s_cin")
        s_mt = sem("s_mt")
        s_lc = sem("s_lc")

        block = ctx.enter_context(nc.Block())

        def heads(l):
            return 8 if l == 2 else 4

        def flags_need(l, gh, b):
            H = heads(l)
            n = gh + 1 + (l * (NG // 2) if l < 2 else 0)
            return flags_in[l // 2][b], n * (16 * H)

        def landed_need(l, gh):
            return (gh + (l * (NG // 2) + 1)) * 16

        def groups(l, eng, body):
            body(0, 0, True, False, False)
            body(0, 1, True, True, False)
            body(1, 0, True, True, True)
            with eng.Fori(1, NG // 2 - 1) as j:
                body(j, 1, True, True, True)
                body(j + 1, 0, True, True, True)
            body(NG // 2 - 1, 1, True, True, True)
            body(NG // 2, 0, False, True, True)
            body(NG // 2, 1, False, False, True)

        def weighed(i, b, second, late):
            if i < GI // 2:
                return (b, i + GI // 2) if late else None
            return (1 - b, i - GI // 2) if second else None

        HALF = [(TILES + 1) // 2, TILES // 2]

        def tiles(eng, *parts):
            deepest = max(lag for _, lag in parts)

            def step(j, bit):
                for f, lag in parts:
                    b = (bit - lag) % 2
                    h = j + (bit - lag - b) // 2
                    t = h * 2 + b
                    if not static(j) or 0 <= t < TILES:
                        f(t, b, h)

            lead = 1 + (deepest + 1) // 2
            for t in range(2 * lead):
                step(t // 2, t % 2)
            with eng.Fori(lead, TILES // 2) as j:
                step(j, 0)
                step(j, 1)
            for t in range(TILES // 2 * 2, TILES + deepest):
                step(t // 2, t % 2)

        def static(v):
            return isinstance(v, int)

        def per_h(ap, H):
            return ap[:, 0:GI * H].rearrange("p (h i) -> p i h", h=H)

        @block.sync
        def _(sp):
            with nc.allow_non_contiguous_dma(reason="one column of dst, once"):
                sp.dma_start(ki[0:CS, 0, 0:CB], dst[:, P - 1:P].rearrange("(j p) o -> p (j o)", p=CS)).then_inc(pre_ld, 16)

            def weights(l):
                if l > 0:
                    sp.wait_ge(acc_done, l * NG * GI)
                with nc.allow_non_contiguous_dma(reason="small weights"):
                    if l < 2:
                        wl, wr, att = ((wl1, wr1, att1), (wl2, wr2, att2))[l]
                        sp.dma_start(W[:, :, 0:D], wl.rearrange("(q p) n -> p q n", p=P)).then_inc(w_in, 16)
                        sp.dma_start(W[:, :, D + 4:2 * D + 4], wr.rearrange("(q p) n -> p q n", p=P)).then_inc(w_in, 16)
                        sp.dma_start(attb[:, 0, :], att.rearrange("h c -> (h c)").partition_broadcast(P)).then_inc(w_in, 16)
                    else:
                        for q in range(2):
                            sp.dma_start(W[:, q, 0:D].rearrange("p (h d) -> p h d", h=8),
                                         w_gat[:, q * P:(q + 1) * P, :].rearrange("h p d -> p h d")).then_inc(w_in, 16)
                        for s in range(2):
                            sp.dma_start(attb[:, s, :].rearrange("p (h d) -> p h d", h=8),
                                         a_gat[:, s * 32:(s + 1) * 32].partition_broadcast(P)).then_inc(w_in, 16)
                    if l > 0:
                        sp.dma_start(bias, (b1, b2)[l - 1].partition_broadcast(P)).then_inc(w_in, 16)

            def attention_blocks(l):
                att = (att1, att2)[l]
                with nc.allow_non_contiguous_dma(reason="256 attention weights as columns"):
                    for h in range(4):
                        r, q = h % 2, h // 2
                        sp.dma_start(attpad[r * 64:(r + 1) * 64, q, GI - 1 + GI * h:GI + GI * h],
                                     att[h:h + 1, :].rearrange("o c -> c o")).then_inc(att_in, 16)

            def rows(t):
                return bass.ds(t * P, P)

            def node_loads(l):
                def load(t, b, h):
                    if not (static(t) and t < 2):
                        if l == 0:
                            sp.wait_ge(h_turned, t - 1)
                        elif l == 1:
                            sp.wait_ge(acc_read, t - 1)
                        else:
                            sp.wait_ge(var_ready, t + ((l - 2) * TILES - 1))
                    if l == 0:
                        sp.dma_start(hbuf[:, b, :], x[rows(t), :]).then_inc(h_in[b], 16)
                    if l in (1, 2):
                        sp.dma_start(own[:, b, :], tab[l - 1][rows(t), :]).then_inc(own_in[b], 16)
                    if l in (2, 3):
                        sp.dma_start(res[:, b, :], (x if l == 2 else hx_dram)[rows(t), :]).then_inc(res_in[b], 16)

                def store(t, b, h):
                    T = t + l * TILES
                    if l == 3:
                        sp.wait_ge(h_ready, t + (2 * TILES + 1))
                        if static(t) and t == TILES - 1:
                            sp.dma_start(out[t * P:N, :], hbuf[0:LAST, b, :]).then_inc(out_stored[b], 16)
                        else:
                            sp.dma_start(out[rows(t), :], hbuf[:, b, :]).then_inc(out_stored[b], 16)
                        return
                    sp.wait_ge(xls_ready, T + 1)
                    if l == 2:
                        sp.dma_start(hx_dram[rows(t), :], hbuf[:, b, :]).then_inc(hx_stored[b], 16)
                    sp.dma_start(tab[l][rows(t), :], xls[:, b, :]).then_inc(stored[b], 16)

                tiles(sp, (load, 0), (store, 2 if l == 3 else 4))
                if l == 3:
                    for b in range(2):
                        sp.wait_ge(out_stored[b], 16 * HALF[b])

            def group_loads(l):
                H = heads(l)

                def body(gh, b):
                    G1 = gh * 2 + (b + l * NG)
                    if not (static(G1) and G1 < 2):
                        sp.wait_ge(s_oh, G1 - 1)
                    k0 = (gh * 2 + b) * GI
                    sp.dma_start(DT[:, b, :], rel_dram[bass.ds(k0, GI), :].rearrange("k e -> (k e)").partition_broadcast(P)).then_inc(relb_in[b], 16)
                    if not (static(G1) and G1 < 2):
                        sp.wait_ge(s_m, G1 - 1)
                    for h in range(H):
                        sp.dma_start(flags[h * GI:(h + 1) * GI, b].rearrange("p f e -> p (f e)"),
                                     flag_dram[bass.ds(k0, GI), :]).then_inc(flags_in[l // 2][b], 16)

                body(0, 0)
                body(0, 1)
                with sp.Fori(1, NG // 2) as j:
                    body(j, 0)
                    body(j, 1)

            weights(0)
            sp.wait_ge(pre_ones, 1)
            attention_blocks(0)
            sp.wait_ge(pre_v, PV_REL)
            sp.dma_start(rel_dram.rearrange("(b p) e -> p b e", p=BS), relbf).then_inc(pre_rel, 16)
            flat = key_dram[1:1 + ITEMS * P].rearrange("(b p e) -> p b e", p=BS, e=P)
            sp.dma_start(flat, key).then_inc(pre_key, 16)
            sp.dma_start(key_dram[0:1], zeros[0:1, 0:1]).then_inc(pre_key, 16)
            sp.dma_start(key_dram[1 + ITEMS * P:2 + ITEMS * P], zeros[0:1, 0:1]).then_inc(pre_key, 16)
            sp.wait_ge(pre_key, 48)
            sp.wait_ge(pre_act, 3)
            sp.dma_start(prev, key_dram[0:ITEMS * P].rearrange("(b p e) -> p b e", p=BS, e=P)).then_inc(pre_shift, 16)
            sp.dma_start(nxt, key_dram[2:2 + ITEMS * P].rearrange("(b p e) -> p b e", p=BS, e=P)).then_inc(pre_shift, 16)
            sp.wait_ge(pre_v, PV_FLAG)
            sp.dma_start(flag_dram.rearrange("(b p) f -> p b f", p=BS), flg.rearrange("p b f e -> p b (f e)")).then_inc(pre_flag, 16)
            node_loads(0)
            sp.wait_ge(pre_rel, 16)
            sp.wait_ge(pre_flag, 16)
            for l in range(3):
                group_loads(l)
                if l < 2:
                    weights(l + 1)
                if l == 0:
                    attention_blocks(1)
                if l == 2:
                    sp.wait_ge(acc_done, 3 * NG * GI)
                    for b in range(2):
                        sp.wait_ge(hx_stored[b], 16 * ((TILES + 1 - b) // 2))
                node_loads(l + 1)

        @block.gpsimd
        def _(pool):
            nc.gpsimd.memset(ones[:], 1.0)
            nc.gpsimd.memset(ones_b[:], 1.0)
            nc.gpsimd.memset(zeros[:], 0.0)
            nc.gpsimd.memset(xls[:], 0.0)
            nc.gpsimd.memset(attpad[:], 0.0).then_inc(pre_ones, 1)
            nc.gpsimd.iota(iota_k_i, [[1, KI]], base=0, channel_multiplier=0)
            nc.gpsimd.iota(ki[:, 1, 0:CB], [[CS, CB]], base=0, channel_multiplier=1)
            nc.gpsimd.iota(ki[:, 2, 0:NB], [[BS, NB]], base=0, channel_multiplier=1).then_inc(pre_iota, 1)
            pool.wait_ge(pre_v, PV_COL)
            for b in range(NB):
                for to, frm in ((g_dst, dst), (g_src, src)):
                    nc.gpsimd.indirect_dma_start(
                        out=to[:, b, :], out_offset=None, in_=frm,
                        in_offset=bass.IndirectOffsetOnAxis(ap=ki[0:BS, 0, b:b + 1], axis=0)).then_inc(pre_gather, 16)

            def carry_wait(word=0):
                nc.gpsimd.tensor_tensor(pool_pad[:, word:word + 1], zeros[:, 0:1], zeros[:, 0:1], ALU.add)

            def node_pool(l):
                cols = slice(D, ROW) if l == 2 else slice(0, D + 4)

                def clear(t, b, h):
                    if not (static(t) and t == 0 and l == 1):
                        pool.wait_ge(acc_zero, t + (l - 1) * TILES)
                    pool.wait_ge(acc_read, t + ((l - 1) * TILES + 1))
                    carry_wait(1)
                    nc.gpsimd.tensor_copy(acc[:, bass.ds(t, 1), :].rearrange("p o r -> p (o r)"), zeros[:]).then_inc(acc_zero, 1)

                def rest(t, b, h):
                    T = t + l * TILES
                    if not (static(T) and T == 0):
                        pool.wait_ge(split_done, T)
                    pool.wait_ge(xr_ready, T + 1)
                    carry_wait(2)
                    high = x3[:, bass.ds(t, 1), 0, cols].rearrange("p o r -> p (o r)")
                    nc.gpsimd.tensor_tensor(r1[:, b, cols], xr[:, b, cols], high, ALU.subtract).then_inc(rest_done, 1)

                def low(t, b, h):
                    T = t + l * TILES
                    pool.wait_ge(middle_done, T + 1)
                    carry_wait(3)
                    _, middle, to = (x3[:, bass.ds(t, 1), s, cols].rearrange("p o r -> p (o r)") for s in range(3))
                    nc.gpsimd.tensor_tensor(to, r1[:, b, cols], middle, ALU.subtract).then_inc(split_done, 1)

                if l:
                    tiles(pool, (clear, 0), (low, 2), (rest, 1))
                else:
                    tiles(pool, (low, 2), (rest, 1))
                pool.wait_ge(mm_done, (l + 1) * TILES)
                pool.wait_ge(split_done, (l + 1) * TILES)
                if l < 2:
                    pool.wait_ge(self_split, l + 1)
                if l > 0:
                    pool.wait_ge(h_ready, l * TILES)
                if l == 2:
                    for b in range(2):
                        pool.wait_ge(hx_stored[b], 16 * HALF[b])
                for b in range(2):
                    pool.wait_ge(stored[b], 16 * HALF[b] * (l + 1))

            def gathers(l):
                def body(gh, b, fresh):
                    G1 = gh * 2 + (b + l * NG)
                    k0 = (gh * 2 + b) * GI
                    def free(upto):
                        pool.wait_ge(seg_done, G1 * GI - (2 * GI - upto))

                    if not fresh:
                        free(4)
                    nc.gpsimd.tensor_copy(idx[:, b, :], src_items[:, bass.ds(k0, GI)]).then_inc(idx_ready, 1)
                    pool.wait_ge(idx_ready, G1 + 1)
                    carry_wait()
                    for i in range(GI):
                        if i % 4 == 0 and i > 0 and not fresh:
                            free(i + 4)
                            carry_wait(1 + i // 4)
                        nc.gpsimd.indirect_dma_start(
                            out=G[:, b, i, :], out_offset=None, in_=tab[l],
                            in_offset=bass.IndirectOffsetOnAxis(ap=idx[:, b, i:i + 1], axis=0)).then_inc(landed[b][i], 16)
                body(0, 0, l == 0)
                body(0, 1, l == 0)
                with pool.Fori(1, NG // 2) as j:
                    body(j, 0, False)
                    body(j, 1, False)

            for l in range(3):
                node_pool(l)
                if l == 0:
                    pool.wait_ge(pre_v, PV_END)
                gathers(l)

        @block.scalar
        def _(act):
            act.wait_ge(pre_pe, 2)
            for b in range(NB):
                ins = nc.scalar.activation(t_row[0:1, b * BS:(b + 1) * BS], pX[0:1, b // FB, (b % FB) * BS:(b % FB + 1) * BS], ACT.Copy)
            ins.then_inc(pre_act, 1)
            act.wait_ge(pre_pe, 3)
            for b in range(NB):
                ins = nc.scalar.activation(rel_items[:, b * BS:(b + 1) * BS], pZ[:, b // FB, (b % FB) * BS:(b % FB + 1) * BS], ACT.Copy)
            ins.then_inc(pre_act, 1)
            act.wait_ge(pre_pe, 4)
            for b in range(NB):
                ins = nc.scalar.activation(src_items[:, b * BS:(b + 1) * BS], pS[:, b // FB, (b % FB) * BS:(b % FB + 1) * BS], ACT.Copy)
            ins.then_inc(pre_act, 1)
            act.wait_ge(pre_pe, 5)
            for b in range(NB):
                at_b = slice((b % FB) * BS, (b % FB + 1) * BS)
                ins = nc.scalar.activation(last_items[:, b * BS:(b + 1) * BS], pS[:, b // FB, at_b], ACT.Copy)
            ins.then_inc(pre_act, 1)

            def node_act(l):
                def now(t, b, h):
                    T = t + l * TILES
                    if l == 1:
                        act.wait_ge(o_ready, t + 1)
                        if not (static(t) and t < 2):
                            act.wait_ge(h_ready, t - 1)
                        nc.scalar.activation(pos[:, b, :], tmp[:, b, :], ACT.Relu)
                        nc.scalar.activation(ex[:, b, :], tmp[:, b, :], ACT.Relu, scale=-1.0).then_inc(elu_neg, 1)
                        act.wait_ge(elu_neg, t + 1)
                        nc.scalar.activation(ex[:, b, :], ex[:, b, :], ACT.Exp, scale=-1.0).then_inc(elu_exp, 1)
                    if l >= 2:
                        act.wait_ge(var_ready, t + ((l - 2) * TILES + 1))
                        nc.scalar.activation(small[:, 4 * b + 3, 2:3], small[:, 4 * b + 3, 1:2], ACT.Sqrt).then_inc(std_ready, 1)

                def turned(t, b, h):
                    act.wait_ge(h_turned, t + (l * TILES + 1))
                    if not (l == 0 and static(t) and t < 2):
                        act.wait_ge(mm_done, t + (l * TILES - 1))
                    nc.scalar.activation(hT[:, b, :], pZ[:, b, 0:D], ACT.Copy).then_inc(ht_ready, 1)

                def products(t, b, h):
                    T = t + l * TILES
                    act.wait_ge(mm_done, T + 1)
                    if not (l == 0 and static(t) and t < 2):
                        act.wait_ge(stored[b], (h + l * HALF[b]) * 16)
                        act.wait_ge(rest_done, T - 1)
                        if l < 2:
                            act.wait_ge(self_ready, T - 1)
                    width = ROW if l == 2 else D + 4
                    nc.scalar.activation(xls[:, b, 0:width], pX[:, b, 0:width], ACT.Copy).then_inc(xls_ready, 1)
                    to, cols = (pX[:, b, ROW:ROW + 8], slice(D, ROW)) if l == 2 else (pS[:, b, 0:D + 4], slice(0, D + 4))
                    nc.scalar.activation(xr[:, b, cols], to, ACT.Copy)
                    nc.scalar.activation(x3[:, bass.ds(t, 1), 0, cols].rearrange("p o r -> p (o r)"), to, ACT.Copy).then_inc(xr_ready, 1)

                def middle(t, b, h):
                    cols = slice(D, ROW) if l == 2 else slice(0, D + 4)
                    act.wait_ge(rest_done, t + (l * TILES + 1))
                    nc.scalar.activation(x3[:, bass.ds(t, 1), 1, cols].rearrange("p o r -> p (o r)"), r1[:, b, cols], ACT.Copy).then_inc(middle_done, 1)

                if l == 0:
                    tiles(act, (turned, 0), (products, 1), (middle, 2))
                elif l < 3:
                    tiles(act, (now, 0), (turned, 1), (products, 2), (middle, 3))
                else:
                    tiles(act, (now, 0))

            def edge_act(l):
                H = heads(l)

                def body(gh, b, first, second, late):
                    G1 = gh * 2 + (b + l * NG)
                    Gq = G1 - 1
                    q0 = (gh * 2 + b) * GI - GI
                    c = 1 - b

                    def relu(i, g):
                        act.wait_ge(zt_done, g * GI + (i + 1))
                        if not (static(g) and g == 0 and i < 2):
                            act.wait_ge(log_done, g * GI + (i - 1))
                        nc.scalar.activation(reluT[:, i % 2, :], pZ[:, i % 2, 0:D], ACT.Relu).then_inc(relu_done, 1)

                    for i in range(GI):
                        if first and l < 2:
                            act.wait_ge(z_done, G1 * GI + (i + 1))
                            nc.scalar.activation(exs[:, b, i, :], pX[:, i % 2, D:ROW], ACT.Copy).then_inc(exs_done, 1)
                            if i >= 1:
                                relu(i - 1, G1)
                        if second and l < 2 and i == 0:
                            relu(GI - 1, Gq)
                        if second and i == 3:
                            rows_of = arow[0:1, :, 0:H * (GI + 1)].rearrange("o r (h k) -> o r h k", h=H)
                            act.wait_ge(s_ab, Gq + 1)
                            ends = pM[0:1, :].rearrange("o (r n) -> o r n", r=4)[:, :, 0:GI * H].rearrange("o r (h k) -> o r h k", h=H)
                            for r in range(2):
                                nc.scalar.activation(rows_of[:, r, :, 1:GI + 1], ends[:, r], ACT.Copy)
                            for r in range(2, 4):
                                ins = nc.scalar.activation(rows_of[:, r, :, 0:GI], ends[:, r], ACT.Copy)
                            ins.then_inc(s_arow, 1)
                        if second and i == 6:
                            act.wait_ge(s_d, Gq + 1)
                            nc.scalar.activation(fr[0:1, 2, 0:H], fr[0:1, 1, 0:H], ACT.Exp).then_inc(s_fx, 1)
                            logs = dif if l == 2 else pM[:, 2 * P:3 * P]
                            nc.scalar.activation(G[:, c, :, D:D + H], per_h(logs, H), ACT.Exp).then_inc(s_w, 1)
                            if l < 2:
                                nc.scalar.activation(dself[:, 0:GI * H], dself[:, 0:GI * H], ACT.Exp).then_inc(s_ws, 1)
                groups(l, act, body)

            for l in range(3):
                node_act(l)
                edge_act(l)
            node_act(3)

        @block.tensor
        def _(pe):
            pe.wait_ge(pre_v, PV_CMP)
            pe.wait_ge(pre_ones, 1)
            for b in range(NB):
                for j in range(CB):
                    mm = nc.tensor.matmul(pM[0:BS, b:b + 1], cmp[:, j, b * BS:(b + 1) * BS], ones_b[0:CS, 0:1],
                                          start=(j == 0), stop=(j == CB - 1))
            mm.then_inc(pre_pe, 1)
            pe.wait_ge(pre_v, PV_COL)

            def row_turn(bank, colf):
                for b in range(NB):
                    mm = nc.tensor.transpose(bank[0:1, b // FB, (b % FB) * BS:(b % FB + 1) * BS], colf(b), ident[0:BS, 0:BS])
                return mm

            def block_turn(bank, tile):
                for b in range(NB):
                    mm = nc.tensor.transpose(bank[:, b // FB, (b % FB) * BS:(b % FB + 1) * BS], tile[:, b, :], ident[0:BS, 0:BS])
                return mm

            row_turn(pX, lambda b: kf[0:BS, b:b + 1]).then_inc(pre_pe, 1)
            pe.wait_ge(pre_v, PV_REL)
            block_turn(pZ, rel).then_inc(pre_pe, 1)
            block_turn(pS, srcf).then_inc(pre_pe, 1)
            pe.wait_ge(pre_v, PV_FLAG)
            pe.wait_ge(pre_act, 3)
            block_turn(pS, lastf).then_inc(pre_pe, 1)
            pe.wait_ge(pre_act, 4)

            def node_pe(l):
                pe.wait_ge(w_ready, l + 1)

                def turn_h(t, b, h):
                    T = t + l * TILES
                    if l == 0:
                        pe.wait_ge(h_in[b], (h + 1) * 16)
                    else:
                        pe.wait_ge(h_ready, t + ((l - 1) * TILES + 1))
                    if not (l == 0 and static(t) and t < 2):
                        pe.wait_ge(ht_ready, T - 1)
                    for q in range(2):
                        mm = nc.tensor.transpose(pZ[:, b, q * P:(q + 1) * P], hbuf[:, b, q * P:(q + 1) * P], ident[:])
                    mm.then_inc(h_turned, 1)

                def products(t, b, h):
                    T = t + l * TILES
                    pe.wait_ge(ht_ready, T + 1)
                    if not (l == 0 and static(t) and t < 2):
                        pe.wait_ge(xr_ready, T - 1)
                    width = 272 if l == 2 else D + 4
                    for q in range(2):
                        mm = nc.tensor.matmul(pX[:, b, 0:width], hT[:, b, q * P:(q + 1) * P], W[:, q, 0:width],
                                              start=(q == 0), stop=(q == 1))
                    if l < 2:
                        for q in range(2):
                            mm = nc.tensor.matmul(pS[:, b, 0:D + 4], hT[:, b, q * P:(q + 1) * P], W[:, q, D + 4:2 * D + 8],
                                                  start=(q == 0), stop=(q == 1))
                    mm.then_inc(mm_done, 1)

                tiles(pe, (turn_h, 0), (products, 1))

            def edge_pe(l):
                H = heads(l)
                pe.wait_ge(split_done, (l + 1) * TILES)
                pe.wait_ge(xr_ready, (l + 1) * TILES)
                if l < 2:
                    pe.wait_ge(self_split, l + 1)
                    pe.wait_ge(s_wl, l + 1)

                def body(gh, b, first, second, late):
                    G1 = gh * 2 + (b + l * NG)
                    Gq = G1 - 1
                    k0 = (gh * 2 + b) * GI
                    c = 1 - b
                    if first:
                        _, tk = nc.values_load_multi_w_load_instructions(
                            t_row[0:1, bass.ds(k0, GI)], engines=(PE,), min_val=0, max_val=TILES - 1,
                            skip_runtime_bounds_check_because="t_k is a tile number by construction")
                        pe.wait_ge(dt_ready, G1 + 1)

                    def expand(i):
                        if l < 2:
                            if not (static(G1) and G1 == 0 and i < 2):
                                pe.wait_ge(z_done, G1 * GI + (i - 1))
                                pe.wait_ge(exs_done, G1 * GI + (i - 1))
                            to, cols = pX[:, i % 2, 0:ROW], slice(0, ROW)
                        else:
                            to, cols = pX[:, b, i * H:(i + 1) * H], slice(D, ROW)
                        for s in range(3):
                            mm = nc.tensor.matmul(to, DT[:, b, i * P:(i + 1) * P],
                                                  x3[:, bass.ds(tk[i], 1), s, cols].rearrange("p o r -> p (o r)"),
                                                  start=(s == 0), stop=(s == 2))
                        mm.then_inc(x_done, 1)

                    def turn(i, g):
                        pe.wait_ge(z_done, g * GI + (i + 1))
                        if not (static(g) and g == 0 and i < 2):
                            pe.wait_ge(relu_done, g * GI + (i - 1))
                        for q in range(2):
                            mm = nc.tensor.transpose(pZ[:, i % 2, q * P:(q + 1) * P], Z[:, i % 2, q * P:(q + 1) * P], ident[:])
                        mm.then_inc(zt_done, 1)

                    def score(i, g):
                        pe.wait_ge(relu_done, g * GI + (i + 1))
                        for q in range(2):
                            mm = nc.tensor.matmul(pL[0:4 * GI, 0:P], attpad[:, q, GI - 1 - i:5 * GI - 1 - i],
                                                  reluT[:, i % 2, q * P:(q + 1) * P], start=(i == 0 and q == 0), stop=False)
                        mm.then_inc(log_done, 1)

                    if first and l < 2:
                        expand(0)
                    for i in range(GI):
                        if first:
                            if l == 2:
                                expand(i)
                            elif i + 1 < GI:
                                expand(i + 1)
                        if second and l < 2 and i == 0:
                            turn(GI - 1, Gq)
                            score(GI - 2, Gq)
                        if second and l < 2 and i == 1:
                            score(GI - 1, Gq)
                            pe.wait_ge(s_l1, Gq + 1)
                            nc.tensor.matmul(pL[0:4 * GI, 0:P], lr[:, 0:4 * GI], ident[:], start=False, stop=True)
                            pe.wait_ge(s_l2, Gq + 1)
                            nc.tensor.transpose(pM[:, 0:P], cand[:], ident[:]).then_inc(s_lt, 1)
                        if second and i == 2 and l == 2:
                            pe.wait_ge(s_cand, Gq + 1)
                            nc.tensor.transpose(pM[:, 0:P], cand[:], ident[:]).then_inc(s_lt, 1)
                        if first and l < 2:
                            if i >= 1:
                                turn(i - 1, G1)
                            if i == 2 and second:
                                pe.wait_ge(s_lc, Gq + 1)
                            if i >= 2:
                                score(i - 2, G1)
                        if second:
                            if i == 3:
                                pe.wait_ge(s_scan, Gq + 1)
                                nc.tensor.transpose(pM[0:1, 0:P], flags[:, c, 2, P - 1:P], ident[:])
                                nc.tensor.transpose(pM[0:1, P:2 * P], F1[:, P - 1:P], ident[:])
                                nc.tensor.transpose(pM[0:1, 2 * P:3 * P], flags[:, c, 3, 0:1], ident[:])
                                nc.tensor.transpose(pM[0:1, 3 * P:4 * P], B1[:, 0:1], ident[:]).then_inc(s_ab, 1)
                            if i == 4:
                                pe.wait_ge(s_cin, Gq + 1)
                                nc.tensor.matmul(pM[:, 0:1], carry_in[0:1, 0, :], ones[0:1, 0:1], start=True, stop=True)
                                nc.tensor.matmul(pM[:, 1:2], carry_in[0:1, 1, :], ones[0:1, 0:1], start=True, stop=True).then_inc(s_carc, 1)
                            if i == 5:
                                pe.wait_ge(s_m, Gq + 1)
                                if l < 2:
                                    nc.tensor.transpose(pM[:, 2 * P:3 * P], dif[:], ident[:])
                                nc.tensor.transpose(pM[:, 3 * P:4 * P], mT[:], ident[:]).then_inc(s_me, 1)
                            if i == 7:
                                pe.wait_ge(s_w, Gq + 1)
                                nc.tensor.matmul(pM[:, 8:8 + H], ones[0:1, :], fr[0:1, 2, 0:H], start=True, stop=True).then_inc(s_fb, 1)
                        at = weighed(i, b, second, late)
                        if at:
                            M = G1 * GI + (i - 3 * GI // 2)
                            pe.wait_ge(wg_done, M + 1)
                            if not (static(M) and M < 2):
                                pe.wait_ge(acc_done, M - 1)
                            nc.tensor.matmul(pS[:, i % 2, 0:ROW], Dm[:, i % 4, :], G[:, at[0], at[1], :], start=True, stop=True).then_inc(seg_done, 1)
                groups(l, pe, body)

            for l in range(3):
                node_pe(l)
                edge_pe(l)

        @block.vector
        def _(dve):
            v = nc.vector
            n_pre = [0]

            def pre(ins, mark=None):
                n_pre[0] += 1
                ins.then_inc(pre_v, 1)
                dve.wait_ge(pre_v, n_pre[0])
                assert mark is None or mark == n_pre[0], (mark, n_pre[0])

            dve.wait_ge(pre_iota, 1)
            pre(v.tensor_copy(kbig, iota_k_i))
            pre(v.tensor_copy(iota_row[:], kbig[:, 0:P]))
            dve.wait_ge(pre_ld, 16)
            pre(v.tensor_single_scalar(ki[0:CS, 0, 0:CB], ki[0:CS, 0, 0:CB], 7, ALU.arith_shift_right))
            pre(v.tensor_copy(kf[0:CS, 0:CB], ki[0:CS, 0, 0:CB]))
            pre(v.tensor_copy(cols[0:CS, 0:CB], ki[0:CS, 1, 0:CB]))
            pre(v.tensor_tensor(kf[0:CS, 0:CB], kf[0:CS, 0:CB], cols[0:CS, 0:CB], ALU.add))
            for j in range(CB):
                ins = v.tensor_scalar(cmp[:, j, :], kbig[0:CS, 0:ITEMS], kf[0:CS, j:j + 1], None, ALU.is_gt)
            pre(ins, PV_CMP)
            pre(v.tensor_copy(iota_part[:], ki[:, 2, 0:1]))
            pre(v.tensor_scalar(ident[:], iota_row[:], iota_part[:, 0:1], None, ALU.is_equal))
            dve.wait_ge(pre_pe, 1)
            pre(v.tensor_copy(ki[0:BS, 0, 0:NB], pM[0:BS, 0:NB]))
            pre(v.tensor_copy(kf[0:BS, 0:NB], ki[0:BS, 2, 0:NB]))
            pre(v.tensor_tensor(kf[0:BS, 0:NB], kf[0:BS, 0:NB], pM[0:BS, 0:NB], ALU.subtract), PV_COL)
            tcol = cols[0:BS, 0:NB]
            pre(v.tensor_scalar(tcol, kf[0:BS, 0:NB], float(P), None, ALU.mult))
            dve.wait_ge(pre_gather, 32 * NB)
            pre(v.tensor_copy(dstf, g_dst))
            pre(v.tensor_copy(srcf, g_src))
            pre(v.tensor_tensor(rel, dstf, tcol.unsqueeze(2).to_broadcast([BS, NB, P]), ALU.subtract))
            pre(v.tensor_scalar(nxt, rel, 0.0, None, ALU.is_ge))
            pre(v.tensor_scalar(key, rel, float(P), None, ALU.is_lt))
            pre(v.tensor_tensor(nxt, nxt, key, ALU.mult))
            pre(v.scalar_tensor_tensor(rel, rel, 1.0, nxt, ALU.add, ALU.mult))
            pre(v.tensor_scalar(rel, rel, -1.0, None, ALU.add))
            pre(v.tensor_copy(relbf, rel))
            pre(v.scalar_tensor_tensor(key, dstf, 1.0, nxt, ALU.add, ALU.mult), PV_REL)
            dve.wait_ge(pre_shift, 32)
            for f, other in ((0, prev), (1, nxt)):
                pre(v.tensor_tensor(dstf, key, other, ALU.is_equal))
                pre(v.tensor_scalar(flg[:, :, f, :], dstf, -1.0, BIG, ALU.add, ALU.mult))
            pre(v.tensor_scalar(lastf, flg[:, :, 1, :], -1.0, None, ALU.is_lt))
            for b in range(NB):
                v.tensor_tensor_scan(flg[:, b, 2, :], flg[:, b, 0, :], flg[:, b, 0, :], 0.0, ALU.min, ALU.min)
                ins = v.tensor_tensor_scan(flg[:, b, 3, ::-1], flg[:, b, 1, ::-1], flg[:, b, 1, ::-1], 0.0, ALU.min, ALU.min)
            pre(ins, PV_FLAG)
            dve.wait_ge(pre_flag, 16)
            dve.wait_ge(pre_rel, 16)
            dve.wait_ge(pre_act, 4)
            pre(v.memset(acc_mem[:, 0:TILES * ROW], 0.0))
            for a in (cand, F1, B1, mT, dif, carry_in, flags):
                v.memset(a[:], 0.0)
            pre(v.memset(arow[:], -BIG), PV_END)

            n_w = [0]

            def wlink(ins):
                n_w[0] += 1
                ins.then_inc(wchain, 1)
                dve.wait_ge(wchain, n_w[0])

            def prepare_weights(l):
                dve.wait_ge(w_in, W_IN[l])
                H = heads(l)
                C = D // H
                for q in range(2):
                    for s in range(2):
                        w = W[:, q, 0:D] if (l == 2 or s == 0) else W[:, q, D + 4:2 * D + 4]
                        o = (D + 8 * s) if l == 2 else (D if s == 0 else 2 * D + 4)
                        wlink(v.tensor_tensor(wtmp, w, attb[:, s if l == 2 else 0, :], ALU.mult))
                        wlink(v.tensor_reduce(W[:, q, o:o + H], wtmp.rearrange("p (h c) -> p h c", h=H), AX.X, ALU.add))
                        if l < 2:
                            wlink(v.tensor_scalar(W[:, q, o:o + H], W[:, q, o:o + H], SLOPE, None, ALU.mult))
                v.tensor_copy(onehot0[:, 0:1], attb[:, 0, 0:1]).then_inc(w_ready, 1)

            def node_dve(l):
                H = heads(l - 1)
                HT = H * TILES
                PER = NODE_STEPS[l]
                base = sum(NODE_STEPS[:l]) * TILES
                n = [0]
                den1, e0, wsx, rd = (nd[:, s, 0:HT].rearrange("p (t h) -> p t h", h=H) for s in range(4))

                def link(ins, t):
                    n[0] += 1
                    ins.then_inc(node_step, 1)
                    dve.wait_ge(node_step, t * PER + (base + n[0]))

                def dlink(ins):
                    n_den[0] += 1
                    ins.then_inc(den_step, 1)
                    dve.wait_ge(den_step, n_den[0])

                def denominators():
                    den = acc[:, :, D:D + H]
                    if l < 3:
                        ws = acc[:, :, D + 4:D + 8]
                        dlink(v.tensor_tensor(den1, den, ws, ALU.add))
                        dlink(v.tensor_scalar(e0, den1, 0.0, None, ALU.is_equal))
                        dlink(v.tensor_tensor(wsx, ws, e0, ALU.add))
                        dlink(v.scalar_tensor_tensor(den1, den1, 1e-16, e0, ALU.add, ALU.add))
                    else:
                        dlink(v.tensor_scalar(e0, den, 0.0, None, ALU.is_equal))
                        dlink(v.tensor_tensor(den1, den, e0, ALU.add))
                    dlink(v.reciprocal(rd, den1))

                def hv(ap):
                    return ap.rearrange("p (h c) -> p h c", h=H)

                def of_tile(ap, t):
                    return ap[:, bass.ds(t, 1), :].rearrange("p o h -> p (o h)").unsqueeze(2).to_broadcast([P, H, D // H])

                def combine(t, b, h):
                    n[0] = 0
                    num = acc[:, bass.ds(t, 1), 0:D].rearrange("p o r -> p (o r)")
                    to = tmp[:, b, :]
                    if not (static(t) and t < 2):
                        dve.wait_ge(h_ready, t + ((l - 1) * TILES - 1))
                    if l < 3:
                        dve.wait_ge(own_in[b], (h + (l - 1) * HALF[b] + 1) * 16)
                        link(v.tensor_tensor(hv(to), hv(own[:, b, 0:D]), of_tile(wsx, t), ALU.mult), t)
                        v.tensor_tensor(to, to, num, ALU.add).then_inc(acc_read, 1)
                        dve.wait_ge(acc_read, t + ((l - 1) * TILES + 1))
                        link(v.tensor_tensor(hv(to), hv(to), of_tile(rd, t), ALU.mult), t)
                    else:
                        v.tensor_tensor(hv(to), hv(num), of_tile(rd, t), ALU.mult).then_inc(acc_read, 1)
                        dve.wait_ge(acc_read, t + (2 * TILES + 1))
                    if l == 1:
                        v.tensor_tensor(to, to, bias, ALU.add).then_inc(o_ready, 1)
                        return
                    if l == 2:
                        link(v.tensor_tensor(to, to, bias, ALU.add), t)
                    dve.wait_ge(res_in[b], (h + (l - 2) * HALF[b] + 1) * 16)
                    link(v.tensor_tensor(to, to, res[:, b, :], ALU.add), t)
                    link(v.bn_stats(small[:, 4 * b, 0:6], to), t)
                    v.memset(small[:, 4 * b + 2, 7:8], 0.0)
                    link(v.bn_aggr(small[:, 4 * b + 1, 0:2], small[:, 4 * b, 0:6]), t)
                    v.tensor_scalar(small[:, 4 * b + 3, 1:2], small[:, 4 * b + 1, 1:2], EPS, None, ALU.add).then_inc(var_ready, 1)
                    assert n[0] == PER, (l, n[0])

                def elu(t, b, h):
                    dve.wait_ge(elu_exp, t + 1)
                    if not (static(t) and t < 2):
                        dve.wait_ge(h_turned, t + (l * TILES - 1))
                    v.scalar_tensor_tensor(hbuf[:, b, :], ex[:, b, :], -1.0, pos[:, b, :], ALU.add, ALU.add).then_inc(h_ready, 1)

                def normalize(t, b, h):
                    U = t + ((l - 2) * TILES + 1)
                    dve.wait_ge(std_ready, U)
                    v.reciprocal(small[:, 4 * b + 3, 0:1], small[:, 4 * b + 3, 2:3]).then_inc(rstd_ready, 1)
                    dve.wait_ge(rstd_ready, U)
                    if not (static(t) and t < 2):
                        if l == 2:
                            dve.wait_ge(h_turned, t + (l * TILES - 1))
                            dve.wait_ge(hx_stored[b], h * 16)
                        else:
                            dve.wait_ge(out_stored[b], h * 16)
                    v.tensor_scalar(hbuf[:, b, :], tmp[:, b, :], small[:, 4 * b + 1, 0:1], small[:, 4 * b + 3, 0:1],
                                    ALU.subtract, ALU.mult).then_inc(h_ready, 1)

                def self_score(t, b, h):
                    T = t + l * TILES
                    for k in range(3):
                        if k == 0:
                            dve.wait_ge(xls_ready, T + 1)
                            dve.wait_ge(xr_ready, T + 1)
                            if not (static(t) and t == 0 and l == 0):
                                dve.wait_ge(self_ready, T)
                            ins = v.tensor_tensor(zs, xls[:, b, 0:D], xr[:, b, 0:D], ALU.add)
                        elif k == 1:
                            ins = v.scalar_tensor_tensor(zs, zs, SLOPE, zs, ALU.mult, ALU.max)
                        else:
                            ins = v.tensor_tensor(zs, zs, attb[:, 0, :], ALU.mult)
                        ins.then_inc(self_step, 1)
                        dve.wait_ge(self_step, T * 3 + (k + 1))
                    v.tensor_reduce(selfs[:, bass.ds(t, 1), :].rearrange("p o h -> p (o h)"), zs.rearrange("p (h c) -> p h c", h=4), AX.X, ALU.add).then_inc(self_ready, 1)

                if l > 0:
                    denominators()
                def split_selfs():
                    dve.wait_ge(self_ready, (l + 1) * TILES)
                    high, middle, low = (x3[:, :, s, D + 4:ROW] for s in range(3))
                    dlink(v.tensor_copy(high, selfs))
                    dlink(v.tensor_tensor(selfs, selfs, high, ALU.subtract))
                    dlink(v.tensor_copy(middle, selfs))
                    v.tensor_tensor(low, selfs, middle, ALU.subtract).then_inc(self_split, 1)

                if l == 0:
                    tiles(dve, (self_score, 0))
                elif l == 1:
                    tiles(dve, (combine, 0), (elu, 1), (self_score, 3))
                else:
                    tiles(dve, (combine, 0), (normalize, 1))
                if l < 2:
                    split_selfs()

            n_den = [0]

            def edge_dve(l):
                H = heads(l)
                HG = H * GI
                RW = H * (GI + 1)
                if l < 2:
                    dve.wait_ge(att_in, 64 * (l + 1))
                    v.tensor_scalar(attpad[:], attpad[:], 1.0 - SLOPE, None, ALU.mult).then_inc(s_wl, 1)
                rows_of = arow[0:1, :, 0:RW].rearrange("o r (h k) -> o r h k", h=H)
                if l > 0:
                    dve.wait_ge(acc_zero, l * TILES)
                    v.memset(arow[:], -BIG).then_inc(pre_acc, 1)
                    dve.wait_ge(pre_acc, l)

                def spread(gh, b):
                    dve.wait_ge(relb_in[b], landed_need(l, gh))
                    v.tensor_scalar(DT[:, b, :], DT[:, b, :], iota_part[:, 0:1], None, ALU.is_equal).then_inc(dt_ready, 1)

                spread(0, 0)

                def body(gh, b, first, second, late):
                    G1 = gh * 2 + (b + l * NG)
                    Gq = G1 - 1
                    c = 1 - b
                    q0 = (gh * 2 + b) * GI - GI
                    qh = gh if b == 1 else gh - 1
                    last_group = static(gh) and gh == NG // 2 - 1 and b == 1
                    w0 = -1 if late else GI // 2
                    w1 = GI if second else GI // 2
                    if second or late:
                        _, tq = nc.values_load_multi_w_load_instructions(
                            t_row[0:1, bass.ds((gh * 2 + b) * GI + (w0 - 3 * GI // 2), w1 - w0)], engines=(DVE,),
                            min_val=0, max_val=TILES - 1,
                            skip_runtime_bounds_check_because="t_k is a tile number by construction")

                    def acc_at(n):
                        return acc[:, bass.ds(tq[n - w0], 1), :].rearrange("p o r -> p (o r)")

                    def add(n):
                        M = G1 * GI + (n - 3 * GI // 2)
                        dve.wait_ge(seg_done, M + 1)
                        if not (static(M) and M == 0):
                            dve.wait_ge(acc_done, M)
                        v.tensor_tensor(acc_at(n), acc_at(n), pS[:, n % 2, 0:ROW], ALU.add).then_inc(acc_done, 1)

                    if late:
                        add(-1)
                    for i in range(GI):
                        if first and l < 2:
                            dve.wait_ge(landed[b][i], landed_need(l, gh))
                            dve.wait_ge(x_done, G1 * GI + (i + 1))
                            if not (static(G1) and G1 == 0 and i < 2):
                                dve.wait_ge(zt_done, G1 * GI + (i - 1))
                            v.tensor_tensor(Z[:, i % 2, :], G[:, b, i, 0:D], pX[:, i % 2, 0:D], ALU.add).then_inc(z_done, 1)
                        if second:
                            if i == 0 and l < 2:
                                dve.wait_ge(exs_done, Gq * GI + GI)
                                v.tensor_tensor(per_h(lr, H), G[:, c, :, D:D + 4], exs[:, c, :, 0:4], ALU.add).then_inc(s_l1, 1)
                                v.tensor_copy(per_h(cand, H), exs[:, c, :, 4:8]).then_inc(s_l2, 1)
                            if i == 2 and l < 2:
                                dve.wait_ge(s_lt, Gq + 1)
                                v.tensor_copy(dself[0:HG, :], pL[0:HG, 0:P]).then_inc(s_lc, 1)
                                dve.wait_ge(s_lc, Gq + 1)
                                v.tensor_tensor(mT[0:HG, :], dself[0:HG, :], pM[0:HG, 0:P], ALU.max).then_inc(s_cand, 1)
                                dve.wait_ge(s_cand, Gq + 1)
                            if i == 2 and l == 2:
                                pl = pX[:, c, 0:HG].rearrange("p (i h) -> p i h", h=H)
                                dve.wait_ge(x_done, Gq * GI + GI)
                                for n in range(GI):
                                    dve.wait_ge(landed[c][n], landed_need(l, qh))
                                v.tensor_tensor(per_h(lr, H), pl, G[:, c, :, D:ROW], ALU.add).then_inc(s_l1, 1)
                                dve.wait_ge(s_l1, Gq + 1)
                                v.scalar_tensor_tensor(cand[:, 0:HG], lr[:, 0:HG], SLOPE, lr[:, 0:HG], ALU.mult, ALU.max).then_inc(s_cand, 1)
                            if i == 3:
                                dve.wait_ge(s_lt, Gq + 1)
                                dve.wait_ge(*flags_need(l, qh, c))
                                cT = mT[0:HG, :] if l < 2 else pM[0:HG, 0:P]
                                v.tensor_tensor_scan(F1[0:HG, :], flags[0:HG, c, 0, :], cT, -BIG, ALU.add, ALU.max)
                                v.tensor_tensor_scan(B1[0:HG, ::-1], flags[0:HG, c, 1, ::-1], cT[:, ::-1], -BIG, ALU.add, ALU.max).then_inc(s_scan, 1)
                            if i == 4:
                                dve.wait_ge(s_arow, Gq + 1)
                                v.tensor_tensor_scan(Fout[0:1, 0:RW], arow[0:1, 0, 0:RW], arow[0:1, 1, 0:RW], -BIG, ALU.add, ALU.max)
                                v.tensor_tensor_scan(Bout[0:1, 0:RW][:, ::-1], arow[0:1, 2, 0:RW][:, ::-1], arow[0:1, 3, 0:RW][:, ::-1],
                                                     -BIG, ALU.add, ALU.max).then_inc(s_car, 1)
                                dve.wait_ge(s_car, Gq + 1)
                                v.tensor_copy(carry_in[0:1, 0, 0:HG].rearrange("o (h k) -> o h k", h=H),
                                              Fout[0:1, 0:RW].rearrange("o (h k) -> o h k", h=H)[:, :, 0:GI])
                                v.tensor_copy(carry_in[0:1, 1, 0:HG].rearrange("o (h k) -> o h k", h=H),
                                              Bout[0:1, 0:RW].rearrange("o (h k) -> o h k", h=H)[:, :, 1:GI + 1]).then_inc(s_cin, 1)
                            if i == 5:
                                dve.wait_ge(s_carc, Gq + 1)
                                v.scalar_tensor_tensor(F1[0:HG, :], flags[0:HG, c, 2, :], pM[0:HG, 0:1], F1[0:HG, :], ALU.add, ALU.max)
                                v.scalar_tensor_tensor(B1[0:HG, :], flags[0:HG, c, 3, :], pM[0:HG, 1:2], B1[0:HG, :], ALU.add, ALU.max).then_inc(s_t, 1)
                                dve.wait_ge(s_t, Gq + 1)
                                if l < 2:
                                    v.tensor_tensor(mT[0:HG, :], F1[0:HG, :], B1[0:HG, :], ALU.max).then_inc(s_mt, 1)
                                    dve.wait_ge(s_mt, Gq + 1)
                                    v.tensor_tensor(dif[0:HG, :], dself[0:HG, :], mT[0:HG, :], ALU.subtract).then_inc(s_m, 1)
                                else:
                                    v.tensor_tensor(mT[0:HG, :], F1[0:HG, :], B1[0:HG, :], ALU.max).then_inc(s_m, 1)
                            if i == 6:
                                dve.wait_ge(s_me, Gq + 1)
                                me = pM[:, 3 * P:3 * P + HG]
                                v.tensor_tensor(fr[0:1, 0, 0:H], rows_of[:, 1, :, 0], me[0:1].rearrange("p (h i) -> p h i", h=H)[:, :, 0], ALU.subtract).then_inc(s_fr, 1)
                                if l == 2:
                                    v.tensor_tensor(dif[:, 0:HG], cand[:, 0:HG], me, ALU.subtract)
                                else:
                                    v.tensor_tensor(per_h(dself, H), exs[:, c, :, 4:8], me.rearrange("p (h i) -> p i h", h=H), ALU.subtract)
                                dve.wait_ge(s_fr, Gq + 1)
                                v.tensor_scalar(fr[0:1, 1, 0:H], fr[0:1, 0, 0:H], 0.0, None, ALU.min).then_inc(s_d, 1)
                            if i == 7:
                                v.tensor_copy(onehot0[:, 0:1], DT[:, c, 0:1]).then_inc(s_oh, 1)
                                dve.wait_ge(s_oh, Gq + 1)
                                v.tensor_scalar(onehot0[:, 1:2], onehot0[:, 0:1], -1.0, 1.0, ALU.mult, ALU.add).then_inc(s_noh, 1)
                                dve.wait_ge(s_noh, Gq + 1)
                                v.tensor_copy(rows_of[:, 1, :, 0], Fout[0:1, 0:RW].rearrange("o (h k) -> o h k", h=H)[:, :, GI]).then_inc(s_cp, 1)
                                if l < 2:
                                    dve.wait_ge(s_ws, Gq + 1)
                                    dve.wait_ge(s_w, Gq + 1)
                                    v.tensor_tensor(G[:, c, :, D + 4:ROW], per_h(dself, H),
                                                    last_items[:, bass.ds(q0, GI)].unsqueeze(2).to_broadcast([P, GI, 4]), ALU.mult)
                                else:
                                    dve.wait_ge(s_w, Gq + 1)
                            if i == 8:
                                if late:
                                    add(GI // 2 - 1)
                                dve.wait_ge(s_fb, Gq + 1)
                                v.tensor_scalar(resc[:, 0:H], pM[:, 8:8 + H], onehot0[:, 0:1], onehot0[:, 1:2], ALU.mult, ALU.add).then_inc(s_sc, 1)
                                dve.wait_ge(s_sc, Gq + 1)
                                if not (static(Gq) and Gq == 0):
                                    dve.wait_ge(acc_done, Gq * GI)
                                a = acc_at(GI // 2)
                                ah = a[:, 0:D].rearrange("p (h d) -> p h d", h=H)
                                v.tensor_tensor(ah, ah, resc[:, 0:H].unsqueeze(2).to_broadcast([P, H, D // H]), ALU.mult)
                                v.tensor_tensor(a[:, D:D + H], a[:, D:D + H], resc[:, 0:H], ALU.mult).then_inc(s_resc, 1)
                                dve.wait_ge(s_resc, Gq + 1)
                        at = weighed(i, b, second, late)
                        if at:
                            M = G1 * GI + (i - 3 * GI // 2)
                            if not (static(M) and M < 4):
                                dve.wait_ge(seg_done, M - 3)
                            v.tensor_scalar(Dm[:, i % 4, :], iota_row[:], rel_items[:, bass.ds((gh * 2 + b) * GI + (i - 3 * GI // 2), 1)], None, ALU.is_equal)
                            gv = G[:, at[0], at[1], 0:D].rearrange("p (h d) -> p h d", h=H)
                            v.tensor_tensor(gv, gv, G[:, at[0], at[1], D:D + H].unsqueeze(2).to_broadcast([P, H, D // H]), ALU.mult).then_inc(wg_done, 1)
                            if i not in (0, GI // 2):
                                add(i - 1)
                        if i == 14 and first and not last_group:
                            spread(gh + b, 1 - b)
                    if late and not second:
                        add(GI // 2 - 1)
                groups(l, dve, body)

            for l in range(3):
                prepare_weights(l)
                node_dve(l)
                edge_dve(l)
                dve.wait_ge(acc_done, (l + 1) * NG * GI)
            node_dve(3)


PV_CMP, PV_COL, PV_REL, PV_FLAG, PV_END = 7, 12, 23, 29, 31
W_IN = [48, 112, 192]
NODE_STEPS = [0, 2, 6, 3]


def kernel(**inputs):
    import numpy as np
    import concourse.bacc as bacc
    from concourse.bass_utils import run_bass_kernel_spmd

    x = np.asarray(inputs["x"])
    src, dst = np.asarray(inputs["src"]), np.asarray(inputs["dst"])
    n, e = x.shape[0], src.shape[0]
    tiles, chunks, _ = sizes(n, e)
    xp = np.zeros((tiles * P, D), x.dtype)
    xp[:n] = x
    srcp = np.zeros((chunks * P,), src.dtype)
    srcp[:e] = src
    dstp = np.full((chunks * P,), tiles * P - 1, dst.dtype)
    dstp[:e] = dst
    arrays = {"x": xp, "src": srcp.reshape(chunks, P), "dst": dstp.reshape(chunks, P)}
    for name in ("L0_gnn_Wl1", "L0_gnn_Wr1", "L0_gnn_att1", "L0_gnn_b1", "L0_gnn_Wl2", "L0_gnn_Wr2", "L0_gnn_att2",
                 "L0_gnn_b2", "L1_gnn_W", "L1_gnn_a"):
        arrays[name] = np.ascontiguousarray(inputs[name])
    nc = bacc.Bacc("TRN2", target_bir_lowering=False, num_devices=1)
    aps = [nc.dram_tensor(f"in_{k}", a.shape, mybir.dt.from_np(a.dtype), kind="ExternalInput").ap() for k, a in arrays.items()]
    out = nc.dram_tensor("out_0", (n, D), F32, kind="ExternalOutput").ap()
    gnn_program(nc, *aps, out)
    r = run_bass_kernel_spmd(nc, [{f"in_{k}": a for k, a in arrays.items()}], core_ids=[0])
    return r.results[0]["out_0"]
```
